# Optimizing a Trainium2 kernel written in Bass

```python
import numpy as np
import jax
import jax.numpy as jnp

def _softmax(x, axis=-1):
    return jax.nn.softmax(x, axis=axis)

def _gelu(x):
    return jax.nn.gelu(x, approximate=True)

def _silu(x):
    return jax.nn.silu(x)

def _sigmoid(x):
    return jax.nn.sigmoid(x)

def _layernorm(x, axis=-1, eps=1e-05):
    m = jnp.mean(x, axis=axis, keepdims=True)
    v = jnp.var(x, axis=axis, keepdims=True)
    return (x - m) / jnp.sqrt(v + eps)

def _scatter_add(tgt, idx, src, axis=0):
    return tgt.at[idx].add(src)

def _segment_sum(src, seg, n):
    return jax.ops.segment_sum(src, seg, n)
kernel_name = 'mk_adj_preln_d2_adj_r2_cf561b'

def setup_inputs(seed: int=0):
    np.random.seed(seed)
    _w = jnp.asarray

    def _rec_inputs():
        import jax
        import jax.numpy as jnp
        _gk = jax.random.key(seed)
        x = 7.22e-05 + 1 * jax.random.normal(jax.random.fold_in(_gk, 1), (4096, 512), jnp.float32)
        _a = jax.random.bernoulli(jax.random.fold_in(_gk, 2), 0.00390625, (4096, 4096))
        _a = jnp.logical_or(_a, jnp.swapaxes(_a, -1, -2))
        _a = jnp.logical_or(_a, jnp.eye(4096, dtype=bool))
        adj = _a.astype(jnp.int32)
        return (x, adj)
    x, adj = _rec_inputs()

    def _L0_gnn_setup():
        import jax, jax.numpy as jnp
        import numpy as np
        N = 4096
        F_IN = 512
        F_OUT = 512
        ALPHA = 0.2
        NEG_INF = -9000000000000000.0
        key = jax.random.key(seed)
        k0, k1, k2, k3, k4 = jax.random.split(key, 5)
        input = jax.random.normal(k0, (N, F_IN), dtype=jnp.float32)
        W = jax.random.normal(k1, (F_IN, F_OUT), dtype=jnp.float32) * np.sqrt(2.0 / (F_IN + F_OUT)).astype(np.float32)
        a1 = jax.random.normal(k2, (F_OUT, 1), dtype=jnp.float32) * 0.05
        a2 = jax.random.normal(k3, (F_OUT, 1), dtype=jnp.float32) * 0.05
        adj = jax.random.randint(k4, (N, N), 0, 2, dtype=jnp.int32)
        return {'input': input, 'adj': adj, 'W': W, 'a1': a1, 'a2': a2}
    _L0_gnn_all = _L0_gnn_setup()
    _L0_gnn_in = {k: v for k, v in _L0_gnn_all.items() if k in ('W', 'a1', 'a2')}
    del _L0_gnn_all

    def _L1_gnn_setup():
        import jax, jax.numpy as jnp
        import numpy as np
        N, D, O = (4096, 512, 512)
        key = jax.random.key(seed)
        ks = jax.random.split(key, 6)
        s = 1.0 / np.sqrt(D)
        x = jax.random.normal(ks[0], (N, D), dtype=jnp.float32)
        adj = jax.random.randint(ks[1], (N, N), 0, 2, dtype=jnp.int32)
        Wf = jax.random.normal(ks[2], (D, D), dtype=jnp.float32) * s
        Wg = jax.random.normal(ks[3], (D, D), dtype=jnp.float32) * s
        W = jax.random.normal(ks[4], (D, O), dtype=jnp.float32) * s
        bf = jnp.zeros((D,), dtype=jnp.float32)
        bg = jnp.zeros((D,), dtype=jnp.float32)
        bW = jnp.zeros((O,), dtype=jnp.float32)
        return {'x': x, 'adj': adj, 'Wf': Wf, 'bf': bf, 'Wg': Wg, 'bg': bg, 'W': W, 'bW': bW}
    _L1_gnn_all = _L1_gnn_setup()
    _L1_gnn_in = {k: v for k, v in _L1_gnn_all.items() if k in ('Wf', 'bf', 'Wg', 'bg', 'W', 'bW')}
    del _L1_gnn_all
    return {'x': x, 'adj': adj, 'L0_gnn_W': _L0_gnn_in['W'], 'L0_gnn_a1': _L0_gnn_in['a1'], 'L0_gnn_a2': _L0_gnn_in['a2'], 'L1_gnn_Wf': _L1_gnn_in['Wf'], 'L1_gnn_bf': _L1_gnn_in['bf'], 'L1_gnn_Wg': _L1_gnn_in['Wg'], 'L1_gnn_bg': _L1_gnn_in['bg'], 'L1_gnn_W': _L1_gnn_in['W'], 'L1_gnn_bW': _L1_gnn_in['bW']}

def reference(x, adj, L0_gnn_W, L0_gnn_a1, L0_gnn_a2, L1_gnn_Wf, L1_gnn_bf, L1_gnn_Wg, L1_gnn_bg, L1_gnn_W, L1_gnn_bW):
    import jax
    import jax.numpy as jnp

    def _L0_gnn_ref(input, adj, W, a1, a2):
        import jax, jax.numpy as jnp
        import numpy as np
        N = 4096
        F_IN = 512
        F_OUT = 512
        ALPHA = 0.2
        NEG_INF = -9000000000000000.0
        h = input @ W
        f1 = h @ a1
        f2 = h @ a2
        e = jax.nn.leaky_relu(f1 + f2.T, negative_slope=ALPHA)
        neg = jnp.asarray(NEG_INF, dtype=e.dtype)
        scores = jnp.where(adj > 0, e, neg)
        attention = jax.nn.softmax(scores, axis=1)
        h_prime = attention @ h
        return jax.nn.relu(h_prime)

    def _L1_gnn_ref(x, adj, Wf, bf, Wg, bg, W, bW):
        import jax, jax.numpy as jnp
        import numpy as np
        N, D, O = (4096, 512, 512)
        NEG = jnp.float32(-9000000000000000.0)
        f = x @ Wf + bf
        g = x @ Wg + bg
        e = jax.nn.relu(f @ g.T)
        scores = jnp.where(adj > 0, e, NEG)
        attention = jax.nn.softmax(scores, axis=1)
        x_W = x @ W + bW
        return attention @ x_W
    h = jnp.maximum(_layernorm(x, axis=-1), 0.0)
    x = x + _L0_gnn_ref(h, adj, L0_gnn_W, L0_gnn_a1, L0_gnn_a2)
    h = jnp.maximum(_layernorm(x, axis=-1), 0.0)
    x = x + _L1_gnn_ref(h, adj, L1_gnn_Wf, L1_gnn_bf, L1_gnn_Wg, L1_gnn_bg, L1_gnn_W, L1_gnn_bW)
    return x

_drawn_inputs = setup_inputs


def setup_inputs(seed=0):
    import zlib

    import numpy as np

    out = dict(_drawn_inputs(seed))
    spreads = {'L1_gnn_bf': (0.0, 0.1), 'L1_gnn_bg': (0.0, 0.419), 'L1_gnn_bW': (0.0, 0.1)}
    factors = {}
    for name, (base, spread) in spreads.items():
        noise = np.random.default_rng([zlib.crc32(name.encode()), seed]).standard_normal(out[name].shape)
        drawn = base * np.exp(spread * noise) if base else spread * noise
        out[name] = jnp.asarray(drawn.astype(out[name].dtype))
    for name, factor in factors.items():
        out[name] = (out[name] * factor).astype(out[name].dtype)
    return out
```

```python
from contextlib import ExitStack

import concourse.bass as bass
from concourse import mybir

F32 = mybir.dt.float32
F16 = mybir.dt.float16
BF16 = mybir.dt.bfloat16
I32 = mybir.dt.int32
ALU = mybir.AluOpType
ACT = mybir.ActivationFunctionType
AX_X = mybir.AxisListType.X

P = 128
SLOPE = 0.2
EPS = 1e-5

H_SCALE = 2.0 ** 10
W_SCALE = 2.0 ** 12
Q_SCALE = 2.0 ** 9
S_SCALE = Q_SCALE * H_SCALE
LN_P_SCALE = 9.704060527839234
MASK = 9e15 * S_SCALE


def graph_layers(nc, x, adj, W0, a1, a2, Wf, bf, Wg, bg, W1, bW, out):
    N, D = x.shape
    NT = N // P
    C = D // P
    NQ = 4
    QW = N // NQ
    JQ = QW // P
    JB = 512
    NJ = N // JB
    BQ = QW // JB

    x1 = nc.dram_tensor("x1_scratch", [N, D], F32, kind="Internal").ap()

    with ExitStack() as ctx:
        def sb(name, shape, dt):
            return ctx.enter_context(nc.sbuf_tensor(name, shape, dt))

        def sem(name):
            return ctx.enter_context(nc.semaphore(name))

        V_hi = sb("V_hi", [P, NT, D], F16)
        V_lo = sb("V_lo", [P, NT, D], F16)
        K_hi = sb("K_hi", [P, C, N], F16)
        K_lo = sb("K_lo", [P, C, N], F16)
        adj_sb = sb("adj_sb", [P, 2, QW], I32)
        mask_sb = sb("mask_sb", [P, 2, QW], BF16)
        score = sb("score", [P, N], F32)
        p_nat = sb("p_nat", [P, 2, 2, QW], F16)
        PT_hi = sb("PT_hi", [P, NT, P], F16)
        PT_lo = sb("PT_lo", [P, NT, P], F16)
        shared = sb("shared", [P, N], F32)
        xres = sb("xres", [P, 2, D], F32)
        work = sb("work", [P, D], F32)
        h_nat = sb("h_nat", [P, 2, D], F16)
        u_row = sb("u_row", [P, D], F32)
        f1 = sb("f1", [P, NT], F32)
        f2 = sb("f2", [P, NT], F32)
        u = sb("u", [P, NT], F32)
        dots = sb("dots", [P, 2], F32)
        q_bias = sb("q_bias", [P, C], F32)
        vec_col = sb("vec_col", [P, 3, C], F32)
        bfbg = sb("bfbg", [P, 1], F32)
        stats = sb("stats", [P, 6], F32)
        mean_var = sb("mean_var", [P, 2], F32)
        ve = sb("ve", [P, 1], F32)
        rstd = sb("rstd", [P, 1], F32)
        shift = sb("shift", [P, 1], F32)
        mhalf = sb("mhalf", [P, 1], F32)
        mask_bias = sb("mask_bias", [P, 1], F32)
        qmax = sb("qmax", [P, NQ], F32)
        rowmax = sb("rowmax", [P, 3], F32)
        neg_max = sb("neg_max", [P, 1], F32)
        qsum = sb("qsum", [P, NQ], F32)
        rowsum = sb("rowsum", [P, 2], F32)
        rinv = sb("rinv", [P, 2], F32)

        w_f32 = score[:, 0:C * D].rearrange("p (c n) -> p c n", c=C)
        w16 = score[:, C * D:2 * C * D].bitcast(F16).rearrange("p (s c n) -> p s c n", s=2, c=C)
        W_hi, W_lo = w16[:, 0], w16[:, 1]
        vecs = adj_sb[:, :, :].rearrange("p a b -> p (a b)").bitcast(F32).rearrange("p (v n) -> p v n", n=D)
        wf_nat = shared[:, 0:C * D].rearrange("p (c n) -> p c n", c=C)
        wg_nat = shared[:, C * D:2 * C * D].rearrange("p (c n) -> p c n", c=C)
        xin = PT_hi[:, :, :].rearrange("p a b -> p (a b)").bitcast(F32).rearrange("p (s n) -> p s n", n=D)
        pn32 = p_nat[:, :, :, :].rearrange("p a b c -> p (a b c)").bitcast(F32)
        diag = pn32[:, 0:D]
        junk = pn32[:, D:2 * D]
        ident = pn32[:, 2 * D:2 * D + P]
        ones = pn32[:, 2 * D + P:2 * D + 2 * P]
        w1_row = pn32[:, 3 * D:4 * D]
        w2_row = PT_lo[:, 0:2 * C, :].rearrange("p a b -> p (a b)").bitcast(F32)
        h_alt = mask_sb[:, 0, :].bitcast(F16).rearrange("p (s n) -> p s n", s=2)
        wl = [PT_hi[:, :, :].rearrange("p a b -> p (a b)").bitcast(F32).rearrange("p (c n) -> p c n", c=C),
              PT_lo[:, :, :].rearrange("p a b -> p (a b)").bitcast(F32).rearrange("p (c n) -> p c n", c=C)]
        ws = p_nat[:, :, :, :].rearrange("p a b (c n) -> p a (b c) n", n=D)
        sh16 = shared[:, :].bitcast(F16).rearrange("p (m s c n) -> p m s c n", m=2, s=2, c=C)
        M_hi, M_lo = sh16[:, 0, 0], sh16[:, 0, 1]
        q_hi, q_lo = sh16[:, 1, 0], sh16[:, 1, 1]

        ps_o = [ctx.enter_context(nc.psum_tensor(f"ps_o{i}", [P, D], F32)) for i in range(2)]
        ps_q = [ctx.enter_context(nc.psum_tensor(f"ps_q{i}", [P, D], F32)) for i in range(2)]
        ps_s = [ctx.enter_context(nc.psum_tensor(f"ps_s{i}", [P, JB], F32)) for i in range(4)]

        params_in = sem("params_in")
        x_in = [sem(f"x_in{i}") for i in range(4)]
        xres_in = [sem(f"xres_in{i}") for i in range(2)]
        adj_in = [sem(f"adj_in{i}") for i in range(2)]
        h0_out = [sem(f"h0_out{i}") for i in range(4)]
        h1_out = sem("h1_out")
        pt_in = [sem(f"pt_in{q}") for q in range(NQ)]
        x1_out = [sem(f"x1_out{i}") for i in range(2)]
        y_out = [sem(f"y_out{i}") for i in range(2)]
        w1_in = sem("w1_in")
        wfg_in = sem("wfg_in")
        wt_in = [sem(f"wt_in{i}") for i in range(2)]
        stood = sem("stood")
        consts = sem("consts")
        zeroed = sem("zeroed")
        tick = sem("tick")
        w_split = sem("w_split")
        w_hi_done = sem("w_hi_done")
        spread_in = sem("spread_in")
        spread_out = sem("spread_out")
        spread_used = sem("spread_used")
        bn_done = sem("bn_done")
        aggr_done = sem("aggr_done")
        ve_done = sem("ve_done")
        rstd_done = sem("rstd_done")
        shift_done = sem("shift_done")
        h_done = sem("h_done")
        h_hi_done = sem("h_hi_done")
        h_lo_done = sem("h_lo_done")
        h_used = sem("h_used")
        dot1_done = sem("dot1_done")
        f_done = sem("f_done")
        v_ready = sem("v_ready")
        v_biased = sem("v_biased")
        v_hi_done = sem("v_hi_done")
        v_lo_done = sem("v_lo_done")
        mask_done = sem("mask_done")
        z_done = sem("z_done")
        max_chain = sem("max_chain")
        y_done = sem("y_done")
        leaky_done = sem("leaky_done")
        exp_done = sem("exp_done")
        p_hi_done = sem("p_hi_done")
        p_lo_done = sem("p_lo_done")
        sum_chain = sem("sum_chain")
        pv_done = sem("pv_done")
        o_relu = sem("o_relu")
        x1_done = sem("x1_done")
        y_final = sem("y_final")
        m_ready = sem("m_ready")
        m_hi_done = sem("m_hi_done")
        m_lo_done = sem("m_lo_done")
        u_done = sem("u_done")
        q_ready = sem("q_ready")
        q_biased = sem("q_biased")
        q_hi_done = sem("q_hi_done")
        q_lo_done = sem("q_lo_done")
        s_ready = sem("s_ready")
        s_relu = sem("s_relu")

        def at_least(eng, semaphore, value):
            if not isinstance(value, int) or value > 0:
                eng.wait_ge(semaphore, value)

        def until(eng, semaphore, value):
            if isinstance(value, int):
                at_least(eng, semaphore, value)
            else:
                eng.wait_ge(semaphore, value).then_inc(stood, 1)

        def paired_tiles(eng, body):
            body(0, 0)
            body(1, 1)
            with eng.Fori(1, NT // 2 - 1, 1) as pair:
                for r in range(2):
                    body(pair * 2 + r, r)
            body(NT - 2, 0)
            body(NT - 1, 1)

        def rows(t, n):
            return t[bass.ds(n * P, P), :]

        block = ctx.enter_context(nc.Block())

        @block.sync
        def _(sp):
            sp.dma_start(w_f32, W0.rearrange("(c p) n -> p c n", p=P)).then_inc(params_in, 16)
            for i, v in enumerate((a1.rearrange("a b -> (a b)"), a2.rearrange("a b -> (a b)"), bf, bg)):
                sp.dma_start(vecs[:, i, :], v.rearrange("(a n) -> a n", a=1).broadcast_to([P, D])).then_inc(params_in, 16)
            sp.dma_start(wf_nat, Wf.rearrange("(c p) n -> p c n", p=P)).then_inc(params_in, 16)
            sp.dma_start(wg_nat, Wg.rearrange("(c p) n -> p c n", p=P)).then_inc(params_in, 16)

            for n in range(4):
                sp.dma_start(xin[:, n, :], rows(x, n)).then_inc(x_in[n], 16)
            def transpose_h0(n, r4):
                until(sp, h_hi_done, n + 1)
                until(sp, h_lo_done, n + 1)
                until(sp, v_ready, n - 3)
                for half, K in ((0, K_hi), (1, K_lo)):
                    sp.dma_start_transpose(K[:, :, bass.ds(n * P, P)],
                                           (h_nat, h_alt)[r4 % 2][:, half, :]).then_inc(h0_out[r4], 16)

            for n in range(4):
                transpose_h0(n, n)
                sp.dma_start(xin[:, n, :], rows(x, n + 4)).then_inc(x_in[n], 16)
            with sp.Fori(1, NT // 4 - 1, 1) as g:
                for r in range(4):
                    transpose_h0(g * 4 + r, r)
                    sp.dma_start(xin[:, r, :], rows(x, g * 4 + (r + 4))).then_inc(x_in[r], 16)
            for n in range(NT - 4, NT):
                transpose_h0(n, n % 4)
            sp.wait_ge(h_used, NT)

            def load_adj(n, q, at):
                until(sp, mask_done, at + q - 1)
                sp.dma_start(adj_sb[:, q % 2, :], adj[bass.ds(n * P, P), q * QW:(q + 1) * QW]).then_inc(adj_in[q % 2], 16)

            def transpose_p(q, at):
                until(sp, p_lo_done, at + q + 1)
                until(sp, pv_done, at - NQ + q + 1)
                for half, PT in ((0, PT_hi), (1, PT_lo)):
                    sp.dma_start_transpose(PT[:, q * JQ:(q + 1) * JQ, :],
                                           p_nat[:, q % 2, half, :]).then_inc(pt_in[q], 16)

            def store_x1(n, r):
                until(sp, x1_done, n + 1)
                sp.dma_start(rows(x1, n), xres[:, r, :]).then_inc(x1_out[r], 16)

            def load_xres(n, r, stored):
                if stored is not None:
                    sp.wait_ge(x1_out[r], stored)
                    until(sp, h_done, NT + n - 1)
                sp.dma_start(xres[:, r, :], rows(x, n)).then_inc(xres_in[r], 16)

            def transpose_h1(n):
                until(sp, h_hi_done, NT + n + 1)
                until(sp, h_lo_done, NT + n + 1)
                for half, K in ((0, K_hi), (1, K_lo)):
                    sp.dma_start_transpose(K[:, :, bass.ds(n * P, P)], h_nat[:, half, :]).then_inc(h1_out, 16)

            load_adj(0, 0, 0)
            load_adj(0, 1, 0)
            load_adj(0, 2, 0)
            load_adj(0, 3, 0)
            load_adj(1, 0, NQ)
            load_adj(1, 1, NQ)
            load_xres(0, 0, None)
            load_xres(1, 1, None)

            def layer0(n, r):
                early = isinstance(n, int) and n < 2
                last = isinstance(n, int) and n == NT - 1
                if isinstance(n, int) and n == 0:
                    sp.wait_ge(v_ready, NT)
                transpose_p(0, n * NQ)
                if not last:
                    load_adj(n + 1, 2, n * NQ + NQ)
                transpose_p(1, n * NQ)
                if not last:
                    load_adj(n + 1, 3, n * NQ + NQ)
                if not early:
                    store_x1(n - 2, r)
                    transpose_h1(n - 2)
                transpose_p(2, n * NQ)
                if not (isinstance(n, int) and n >= NT - 2):
                    load_adj(n + 2, 0, n * NQ + 2 * NQ)
                transpose_p(3, n * NQ)
                if not (isinstance(n, int) and n >= NT - 2):
                    load_adj(n + 2, 1, n * NQ + 2 * NQ)
                if not early:
                    load_xres(n, r, (n - r) * 8)

            paired_tiles(sp, layer0)

            sp.wait_ge(p_lo_done, NT * NQ)
            sp.dma_start(w_f32, W1.rearrange("(c p) n -> p c n", p=P)).then_inc(w1_in, 16)
            sp.wait_ge(mask_done, NT * NQ)
            sp.dma_start(vecs[:, 2, :], bW.rearrange("(a n) -> a n", a=1).broadcast_to([P, D])).then_inc(w1_in, 16)
            for n in range(NT - 2, NT):
                store_x1(n, n % 2)
                transpose_h1(n)
            sp.wait_ge(pv_done, NT * NQ)
            for i, w in enumerate((Wf, Wg)):
                sp.dma_start(wl[i], w.rearrange("(c p) n -> p c n", p=P)).then_inc(wfg_in, 16)
            for i in range(2):
                sp.wait_ge(w_split, 2 + i + 1)
                for half in range(2):
                    for c in range(C):
                        sp.dma_start_transpose(sh16[:, i, half, :, c * P:(c + 1) * P],
                                               ws[:, half, c, :]).then_inc(wt_in[i], 16)

            B = NT * NQ
            sp.wait_ge(v_biased, NT)
            for q in range(2):
                sp.dma_start(adj_sb[:, q, :], adj[0:P, q * QW:(q + 1) * QW]).then_inc(adj_in[q], 16)
            load_adj(0, 2, B)
            load_adj(0, 3, B)
            load_adj(1, 0, B + NQ)
            load_adj(1, 1, B + NQ)
            for r in range(2):
                sp.wait_ge(x1_out[r], NT // 2 * 16)
                sp.wait_ge(h_done, 2 * NT)
                sp.dma_start(xres[:, r, :], x1[r * P:(r + 1) * P, :]).then_inc(xres_in[r], 16)

            def layer1(n, r):
                for q in range(NQ):
                    transpose_p(q, B + n * NQ)
                if not (isinstance(n, int) and n == NT - 1):
                    load_adj(n + 1, 2, B + n * NQ + NQ)
                    load_adj(n + 1, 3, B + n * NQ + NQ)
                if not (isinstance(n, int) and n == 0):
                    m, s = n - 1, 1 - r
                    until(sp, y_final, n)
                    sp.dma_start(rows(out, m), xres[:, s, :]).then_inc(y_out[s], 16)
                if not (isinstance(n, int) and n >= NT - 2):
                    load_adj(n + 2, 0, B + n * NQ + 2 * NQ)
                    load_adj(n + 2, 1, B + n * NQ + 2 * NQ)
                if not (isinstance(n, int) and (n == 0 or n == NT - 1)):
                    m, s = n - 1, 1 - r
                    sp.wait_ge(y_out[s], (m - s) * 8 + 16)
                    sp.dma_start(xres[:, s, :], rows(x1, n + 1)).then_inc(xres_in[s], 16)

            paired_tiles(sp, layer1)
            sp.wait_ge(y_final, NT)
            sp.dma_start(rows(out, NT - 1), xres[:, 1, :]).then_inc(y_out[1], 16)
            for r in range(2):
                sp.wait_ge(y_out[r], NT // 2 * 16)

        @block.gpsimd
        def _(pool):
            nc.gpsimd.memset(ident, 0.0).then_inc(zeroed, 1)
            nc.gpsimd.memset(ones, 1.0).then_inc(consts, 1)
            nc.gpsimd.memset(mhalf[:, :], -0.5).then_inc(zeroed, 1)
            nc.gpsimd.memset(mask_bias[:, :], MASK).then_inc(consts, 1)
            pool.wait_ge(zeroed, 2)
            nc.gpsimd.affine_select(out=ident, in_=ident, compare_op=ALU.not_equal, fill=1.0, base=0,
                                    pattern=[[-1, P]], channel_multiplier=1).then_inc(consts, 1)
            def inverse_deviation(n):
                until(pool, aggr_done, n + 1)
                nc.gpsimd.tensor_scalar(ve[:, :], mean_var[:, 1:2], EPS, H_SCALE ** -2,
                                        ALU.add, ALU.mult).then_inc(ve_done, 1)
                pool.wait_ge(ve_done, n + 1)
                at_least(pool, h_done, n)
                nc.gpsimd.tensor_tensor(rstd[:, :], ve[:, :], mhalf[:, :], ALU.pow).then_inc(rstd_done, 1)

            inverse_deviation(0)
            with pool.Fori(1, 2 * NT, 1) as n:
                inverse_deviation(n)

        @block.scalar
        def _(act):
            def split_hi(w, hi, loaded, value, done):
                act.wait_ge(loaded, value)
                nc.scalar.mul(hi, w, W_SCALE).then_inc(done, 1)

            split_hi(w_f32, W_hi, params_in, 7 * 16, w_hi_done)

            def normalise(n, xt, t, hn):
                act.wait_ge(shift_done, n + 1)
                nc.scalar.activation(t, xt, ACT.Relu, bias=shift[:, :], scale=rstd[:, :]).then_inc(h_done, 1)
                act.wait_ge(h_done, n + 1)
                nc.scalar.copy(hn[:, 0, :], t).then_inc(h_hi_done, 1)

            def value_hi(n, r):
                act.wait_ge(v_ready, n + 1)
                nc.scalar.activation(V_hi[:, bass.ds(n, 1), :], ps_o[r][:, :].rearrange("p (a n) -> p a n", a=1),
                                     ACT.Copy, scale=1.0 / W_SCALE).then_inc(v_hi_done, 1)

            def ln0(n, r4):
                r = r4 % 2
                first = isinstance(n, int)
                act.wait_ge(shift_done, n + 1)
                if not (first and n < 2):
                    act.wait_ge(h_used, n - 1)
                nc.scalar.activation((work[:, :], xres[:, 0, :])[r], xin[:, r4, :], ACT.Relu,
                                     bias=shift[:, :], scale=rstd[:, :]).then_inc(h_done, 1)
                act.wait_ge(h_done, n + 1)
                if not (first and n < 2):
                    act.wait_ge(h0_out[(r4 + 2) % 4], (n - 2 - (r4 + 2) % 4) * 8 + 32)
                nc.scalar.copy((h_nat, h_alt)[r][:, 0, :], (work[:, :], xres[:, 0, :])[r]).then_inc(h_hi_done, 1)
                if not (first and n < 2):
                    value_hi(n - 2, r)

            for n in range(4):
                ln0(n, n)
            with act.Fori(1, NT // 4, 1) as g:
                for r in range(4):
                    ln0(g * 4 + r, r)
            value_hi(NT - 2, 0)
            value_hi(NT - 1, 1)

            def mask(q, at):
                act.wait_ge(adj_in[q % 2], at * 8 + 16 * (q // 2 + 1))
                at_least(act, z_done, at + q - 1)
                nc.scalar.activation(mask_sb[:, q % 2, :], adj_sb[:, q % 2, :], ACT.Relu,
                                     bias=mask_bias[:, :], scale=-MASK).then_inc(mask_done, 1)

            def exp_quarter(q, at, scale):
                nc.scalar.activation(score[:, q * QW:(q + 1) * QW], score[:, q * QW:(q + 1) * QW], ACT.Exp,
                                     bias=neg_max[:, :], scale=scale,
                                     accum_out=qsum[:, q:q + 1]).then_inc(exp_done, 1)

            def p_hi(q, at):
                act.wait_ge(exp_done, at + q + 1)
                if q >= 2:
                    act.wait_ge(pt_in[q - 2], at * 8 + 32)
                else:
                    at_least(act, pt_in[q + 2], at * 8)
                nc.scalar.copy(p_nat[:, q % 2, 0, :], score[:, q * QW:(q + 1) * QW]).then_inc(p_hi_done, 1)

            def relu_out(n, r):
                act.wait_ge(pv_done, n * NQ + NQ)
                act.wait_ge(sum_chain, 3 * n + 3)
                act.wait_ge(h_used, NT + n)
                nc.scalar.activation(work[:, :], ps_o[r][:, :], ACT.Relu, scale=rinv[:, r:r + 1]).then_inc(o_relu, 1)

            def norm1(n, r):
                act.wait_ge(shift_done, NT + n + 1)
                nc.scalar.activation(work[:, :], xres[:, r, :], ACT.Relu, bias=shift[:, :],
                                     scale=rstd[:, :]).then_inc(h_done, 1)
                act.wait_ge(h_done, NT + n + 1)
                at_least(act, h1_out, n * 32)
                nc.scalar.copy(h_nat[:, 0, :], work[:, :]).then_inc(h_hi_done, 1)

            for q in range(NQ):
                mask(q, 0)

            def layer0(n, r):
                early = isinstance(n, int) and n < 2
                last = isinstance(n, int) and n == NT - 1
                at = n * NQ
                if not early:
                    relu_out(n - 2, r)
                at_least(act, sum_chain, 3 * n)
                for q in range(2):
                    act.wait_ge(leaky_done, at + q + 1)
                    exp_quarter(q, at, 1.0)
                p_hi(0, at)
                if not last:
                    mask(0, at + NQ)
                for q in range(2, NQ):
                    act.wait_ge(leaky_done, at + q + 1)
                    exp_quarter(q, at, 1.0)
                    p_hi(q - 1, at)
                    if q == 2 and not last:
                        mask(1, at + NQ)
                if not early:
                    norm1(n - 2, r)
                if not last:
                    mask(2, at + NQ)
                p_hi(3, at)
                if not last:
                    mask(3, at + NQ)

            paired_tiles(act, layer0)

            split_hi(w_f32, W_hi, w1_in, 2 * 16, w_hi_done)
            for n in range(NT - 2, NT):
                relu_out(n, n % 2)
                norm1(n, n % 2)

            def value_hi1(n, r):
                act.wait_ge(v_biased, n + 1)
                nc.scalar.copy(V_hi[:, bass.ds(n, 1), :],
                               ps_o[r][:, :].rearrange("p (a n) -> p a n", a=1)).then_inc(v_hi_done, 1)

            def values1(lo, hi):
                with act.Fori(lo // 2, hi // 2, 1) as pair:
                    for r in range(2):
                        value_hi1(pair * 2 + r, r)

            def weight_hi(i):
                act.wait_ge(wfg_in, 2 * 16)
                if i:
                    act.wait_ge(wt_in[0], 8 * 16)
                nc.scalar.mul(ws[:, 0], wl[i], W_SCALE).then_inc(w_hi_done, 1)

            values1(0, NT // 2)
            weight_hi(0)
            values1(NT // 2, NT // 2 + 8)
            weight_hi(1)
            values1(NT // 2 + 8, NT)
            for c in range(C):
                act.wait_ge(m_ready, C)
                nc.scalar.activation(M_hi[:, c, :], ps_s[c][:, :], ACT.Copy, scale=1.0 / W_SCALE).then_inc(m_hi_done, 1)

            def query_hi(g):
                for c in range(C):
                    act.wait_ge(q_biased, g * C + c + 1)
                    nc.scalar.copy(q_hi[:, c, :], ps_q[c % 2][:, :]).then_inc(q_hi_done, 1)

            B = NT * NQ

            def relu_scores(n):
                at = B + n * NQ
                for q in range(NQ):
                    mask(q, at)
                    act.wait_ge(p_lo_done, at - NQ + q + 1)
                    for b in range(BQ):
                        j = q * BQ + b
                        until(act, s_ready, n * NJ + j + 1)
                        nc.scalar.activation(score[:, j * JB:(j + 1) * JB], ps_s[j % 4][:, :], ACT.Relu,
                                             bias=u[:, bass.ds(n, 1)]).then_inc(s_relu, 1)

            def layer1(n, r4, queries):
                at = B + n * NQ
                act.wait_ge(sum_chain, 3 * NT + 3 * n)
                act.wait_ge(max_chain, 4 * NT + 2 * n + 2)
                for q in range(2):
                    exp_quarter(q, at, 1.0 / S_SCALE)
                p_hi(0, at)
                for q in range(2, NQ):
                    exp_quarter(q, at, 1.0 / S_SCALE)
                    p_hi(q - 1, at)
                p_hi(3, at)
                if not (isinstance(n, int) and n == NT - 1):
                    relu_scores(n + 1)
                if queries is not None:
                    query_hi(queries)

            query_hi(0)
            act.wait_ge(u_done, 1)
            relu_scores(0)
            with act.Fori(0, NT // 4 - 1, 1) as g:
                for r in range(4):
                    layer1(g * 4 + r, r, g + 1 if r == 2 else None)
            for r in range(4):
                layer1(NT - 4 + r, r, None)

        @block.vector
        def _(dve):
            ticks = [0]

            def ticked(ins):
                ins.then_inc(tick, 1)
                ticks[0] += 1
                return ticks[0]

            def split_lo(w, hi, lo):
                return nc.vector.scalar_tensor_tensor(out=lo, in0=w, scalar=W_SCALE, in1=hi,
                                                      op0=ALU.mult, op1=ALU.subtract)

            def dot(o, a, b, scale, acc):
                return nc.vector.tensor_tensor_reduce(out=o, in0=a, in1=b, scale=scale, scalar=0.0,
                                                      op0=ALU.mult, op1=ALU.add, accum_out=acc)

            dve.wait_ge(params_in, 7 * 16)
            t = 0
            for v, (w, vec) in enumerate(((w_f32, 0), (w_f32, 1), (wf_nat, 3), (wg_nat, 2))):
                for c in range(C):
                    acc = vec_col[:, v, c:c + 1] if v < 3 else q_bias[:, c:c + 1]
                    at_least(dve, tick, t)
                    t = ticked(dot(junk, w[:, c, :], vecs[:, vec, :], Q_SCALE if v == 3 else 1.0, acc))
            dve.wait_ge(tick, t)
            t = ticked(dot(junk, vecs[:, 2, :], vecs[:, 3, :], S_SCALE, bfbg[:, :]))
            dve.wait_ge(w_hi_done, 1)
            split_lo(w_f32, W_hi, W_lo).then_inc(w_split, 1)
            dve.wait_ge(tick, t)
            dve.wait_ge(consts, 3)

            def spread(col, dst, i):
                at_least(dve, spread_out, i)
                for c in range(C):
                    last = nc.vector.tensor_scalar(diag[:, c * P:(c + 1) * P], ident, col[:, c:c + 1], None, ALU.mult)
                last.then_inc(spread_in, 1)
                dve.wait_ge(spread_out, i + 1)
                nc.vector.tensor_copy(dst, ps_q[0][:, :]).then_inc(spread_used, 1)

            for v, dst in enumerate((w1_row, w2_row, u_row[:, :])):
                spread(vec_col[:, v, :], dst, v)
            dve.wait_ge(spread_used, 3)

            def statistics(xt, n):
                nc.vector.bn_stats(stats[:, :], xt).then_inc(bn_done, 1)
                dve.wait_ge(bn_done, n + 1)
                until(dve, rstd_done, n)
                nc.vector.bn_aggr(mean_var[:, :], stats[:, :]).then_inc(aggr_done, 1)

            def make_shift(n):
                dve.wait_ge(rstd_done, n + 1)
                at_least(dve, h_done, n)
                nc.vector.scalar_tensor_tensor(out=shift[:, :], in0=mean_var[:, 0:1], scalar=-1.0,
                                               in1=rstd[:, :], op0=ALU.mult, op1=ALU.mult).then_inc(shift_done, 1)

            def value_lo(n, r, scale):
                at = n if scale != 1.0 else n + NT
                dve.wait_ge(v_hi_done, at + 1)
                nc.vector.scalar_tensor_tensor(out=V_lo[:, bass.ds(n, 1), :],
                                               in0=ps_o[r][:, :].rearrange("p (a n) -> p a n", a=1), scalar=scale,
                                               in1=V_hi[:, bass.ds(n, 1), :],
                                               op0=ALU.mult, op1=ALU.subtract).then_inc(v_lo_done, 1)

            def ln0(n, r4):
                first = isinstance(n, int)
                dve.wait_ge(x_in[r4], (n - r4) * 4 + 16)
                statistics(xin[:, r4, :], n)
                if not (first and n == 0):
                    products0(n - 1, (r4 - 1) % 4)
                make_shift(n)
                if not (first and n < 3):
                    value_lo(n - 3, (r4 + 1) % 2, 1.0 / W_SCALE)

            def products0(n, r4):
                r = r4 % 2
                t = (work[:, :], xres[:, 0, :])[r]
                hn = (h_nat, h_alt)[r]
                dve.wait_ge(h_hi_done, n + 1)
                nc.vector.tensor_tensor(hn[:, 1, :], t, hn[:, 0, :], ALU.subtract).then_inc(h_lo_done, 1)
                at_least(dve, f_done, n)
                dot(junk, t, w1_row, 1.0 / H_SCALE, dots[:, 0:1]).then_inc(dot1_done, 1)
                dve.wait_ge(dot1_done, n + 1)
                dot(junk, t, w2_row, 1.0 / H_SCALE, dots[:, 1:2]).then_inc(h_used, 1)
                dve.wait_ge(h_used, n + 1)
                nc.vector.tensor_copy(f1[:, bass.ds(n, 1)], dots[:, 0:1])
                nc.vector.tensor_copy(f2[:, bass.ds(n, 1)], dots[:, 1:2]).then_inc(f_done, 1)

            for n in range(4):
                ln0(n, n)
            with dve.Fori(1, NT // 4, 1) as g:
                for r in range(4):
                    ln0(g * 4 + r, r)
            products0(NT - 1, 3)
            for n in range(NT - 3, NT):
                value_lo(n, n % 2, 1.0 / W_SCALE)

            dve.wait_ge(f_done, NT)
            for g in range(NT // C):
                spread(f2[:, g * C:(g + 1) * C], shared[:, g * D:(g + 1) * D], 3 + g)
            dve.wait_ge(spread_used, 3 + NT // C)

            def masked(q, at):
                at_least(dve, p_lo_done, at - NQ + q + 1)
                until(dve, mask_done, at + q + 1)
                s = slice(q * QW, (q + 1) * QW)
                nc.vector.tensor_tensor_reduce(out=score[:, s], in0=shared[:, s], in1=mask_sb[:, q % 2, :], scale=1.0,
                                               scalar=-3e38, op0=ALU.subtract, op1=ALU.max,
                                               accum_out=qmax[:, q:q + 1]).then_inc(z_done, 1)

            def maximum0(n):
                dve.wait_ge(z_done, n * NQ + NQ)
                nc.vector.reduce_max(rowmax[:, 0:1], qmax[:, :], AX_X).then_inc(max_chain, 1)
                dve.wait_ge(max_chain, 4 * n + 1)
                nc.vector.tensor_scalar(rowmax[:, 1:2], rowmax[:, 0:1], f1[:, bass.ds(n, 1)], None,
                                        ALU.add).then_inc(max_chain, 1)
                dve.wait_ge(max_chain, 4 * n + 2)
                nc.vector.scalar_tensor_tensor(out=rowmax[:, 2:3], in0=rowmax[:, 1:2], scalar=SLOPE,
                                               in1=rowmax[:, 1:2], op0=ALU.mult, op1=ALU.max).then_inc(max_chain, 1)
                dve.wait_ge(max_chain, 4 * n + 3)
                at_least(dve, exp_done, n * NQ)
                nc.vector.tensor_scalar(neg_max[:, :], rowmax[:, 2:3], -1.0, LN_P_SCALE,
                                        ALU.mult, ALU.add).then_inc(max_chain, 1)

            def add_f1(n, q):
                s = slice(q * QW, (q + 1) * QW)
                nc.vector.tensor_scalar(score[:, s], score[:, s], f1[:, bass.ds(n, 1)], None, ALU.add).then_inc(y_done, 1)

            def leaky(n, q):
                s = slice(q * QW, (q + 1) * QW)
                dve.wait_ge(y_done, n * NQ + q + 1)
                nc.vector.scalar_tensor_tensor(out=score[:, s], in0=score[:, s], scalar=SLOPE, in1=score[:, s],
                                               op0=ALU.mult, op1=ALU.max).then_inc(leaky_done, 1)

            def p_lo(q, at):
                dve.wait_ge(p_hi_done, at + q + 1)
                nc.vector.tensor_tensor(p_nat[:, q % 2, 1, :], score[:, q * QW:(q + 1) * QW], p_nat[:, q % 2, 0, :],
                                        ALU.subtract).then_inc(p_lo_done, 1)

            def inverse_sum(n, r):
                dve.wait_ge(exp_done, n * NQ + NQ)
                nc.vector.reduce_sum(rowsum[:, 0:1], qsum[:, :], AX_X).then_inc(sum_chain, 1)
                dve.wait_ge(sum_chain, 3 * n + 1)
                nc.vector.tensor_scalar(rowsum[:, 1:2], rowsum[:, 0:1], H_SCALE, None, ALU.mult).then_inc(sum_chain, 1)
                dve.wait_ge(sum_chain, 3 * n + 2)
                nc.vector.reciprocal(rinv[:, r:r + 1], rowsum[:, 1:2]).then_inc(sum_chain, 1)

            def residual0(n, r):
                dve.wait_ge(o_relu, n + 1)
                dve.wait_ge(xres_in[r], (n - r) * 8 + 16)
                nc.vector.tensor_tensor(xres[:, r, :], xres[:, r, :], work[:, :], ALU.add).then_inc(x1_done, 1)
                dve.wait_ge(x1_done, n + 1)
                statistics(xres[:, r, :], NT + n)

            def products1(n):
                dve.wait_ge(h_hi_done, NT + n + 1)
                nc.vector.tensor_tensor(h_nat[:, 1, :], work[:, :], h_nat[:, 0, :], ALU.subtract).then_inc(h_lo_done, 1)
                dve.wait_ge(h_lo_done, NT + n + 1)
                dot(work[:, :], work[:, :], u_row[:, :], S_SCALE / H_SCALE, dots[:, 0:1]).then_inc(h_used, 1)
                dve.wait_ge(h_used, NT + n + 1)
                nc.vector.tensor_copy(u[:, bass.ds(n, 1)], dots[:, 0:1]).then_inc(f_done, 1)

            for q in range(NQ):
                masked(q, 0)
            maximum0(0)

            def layer0(n, r):
                early = isinstance(n, int) and n < 2
                last = isinstance(n, int) and n == NT - 1
                at = n * NQ
                add_f1(n, 0)
                add_f1(n, 1)
                leaky(n, 0)
                dve.wait_ge(max_chain, 4 * n + 4)
                add_f1(n, 2)
                leaky(n, 1)
                add_f1(n, 3)
                leaky(n, 2)
                leaky(n, 3)
                if not early:
                    residual0(n - 2, r)
                p_lo(0, at)
                if not early:
                    make_shift(NT + n - 2)
                p_lo(1, at)
                if not last:
                    masked(0, at + NQ)
                p_lo(2, at)
                if not last:
                    masked(1, at + NQ)
                if not early:
                    products1(n - 2)
                p_lo(3, at)
                if not last:
                    masked(2, at + NQ)
                    masked(3, at + NQ)
                inverse_sum(n, r)
                if not last:
                    maximum0(n + 1)

            paired_tiles(dve, layer0)

            dve.wait_ge(w1_in, 2 * 16)
            dve.wait_ge(w_hi_done, 2)
            split_lo(w_f32, W_hi, W_lo).then_inc(w_split, 1)
            t = ticked(nc.vector.tensor_scalar(vecs[:, 2, :], vecs[:, 2, :], H_SCALE, None, ALU.mult))
            dve.wait_ge(tick, t)
            for n in range(NT - 2, NT):
                residual0(n, n % 2)
                make_shift(NT + n)
                products1(n)
            dve.wait_ge(f_done, 2 * NT)
            nc.vector.tensor_scalar(u[:, :], u[:, :], bfbg[:, :], None, ALU.add).then_inc(u_done, 1)

            def value_bias(n, r):
                dve.wait_ge(v_ready, NT + n + 1)
                nc.vector.scalar_tensor_tensor(out=ps_o[r][:, :], in0=ps_o[r][:, :], scalar=1.0 / W_SCALE,
                                               in1=vecs[:, 2, :], op0=ALU.mult, op1=ALU.add).then_inc(v_biased, 1)

            def value_tiles(lo, hi):
                with dve.Fori(lo // 2, hi // 2, 1) as pair:
                    for r in range(2):
                        value_bias(pair * 2 + r, r)
                        value_lo(pair * 2 + r, r, 1.0)

            def weight_lo(i):
                dve.wait_ge(w_hi_done, 3 + i)
                split_lo(wl[i], ws[:, 0], ws[:, 1]).then_inc(w_split, 1)

            value_tiles(0, NT // 2)
            weight_lo(0)
            value_tiles(NT // 2, NT // 2 + 8)
            weight_lo(1)
            value_tiles(NT // 2 + 8, NT)
            for c in range(C):
                dve.wait_ge(m_hi_done, c + 1)
                nc.vector.scalar_tensor_tensor(out=M_lo[:, c, :], in0=ps_s[c][:, :], scalar=1.0 / W_SCALE,
                                               in1=M_hi[:, c, :], op0=ALU.mult, op1=ALU.subtract).then_inc(m_lo_done, 1)

            def query_lo(g):
                for c in range(C):
                    dve.wait_ge(q_ready, g * C + c + 1)
                    nc.vector.tensor_scalar(ps_q[c % 2][:, :], ps_q[c % 2][:, :], Q_SCALE / (H_SCALE * W_SCALE),
                                            q_bias[:, c:c + 1], ALU.mult, ALU.add).then_inc(q_biased, 1)
                    dve.wait_ge(q_hi_done, g * C + c + 1)
                    nc.vector.tensor_tensor(q_lo[:, c, :], ps_q[c % 2][:, :], q_hi[:, c, :],
                                            ALU.subtract).then_inc(q_lo_done, 1)

            B = NT * NQ

            def masked1(n):
                at = B + n * NQ
                for q in range(NQ):
                    dve.wait_ge(s_relu, n * NJ + (q + 1) * BQ)
                    until(dve, mask_done, at + q + 1)
                    s = slice(q * QW, (q + 1) * QW)
                    nc.vector.tensor_tensor_reduce(out=score[:, s], in0=score[:, s], in1=mask_sb[:, q % 2, :],
                                                   scale=1.0, scalar=-3e38, op0=ALU.subtract, op1=ALU.max,
                                                   accum_out=qmax[:, q:q + 1]).then_inc(z_done, 1)
                dve.wait_ge(z_done, at + NQ)
                nc.vector.reduce_max(rowmax[:, 0:1], qmax[:, :], AX_X).then_inc(max_chain, 1)
                dve.wait_ge(max_chain, 4 * NT + 2 * n + 1)
                dve.wait_ge(exp_done, at)
                nc.vector.tensor_scalar(neg_max[:, :], rowmax[:, 0:1], -1.0 / S_SCALE, LN_P_SCALE,
                                        ALU.mult, ALU.add).then_inc(max_chain, 1)

            def final(n, r):
                dve.wait_ge(pv_done, B + n * NQ + NQ)
                dve.wait_ge(xres_in[r], NT // 2 * 16 + (n - r) * 8 + 16)
                nc.vector.scalar_tensor_tensor(out=xres[:, r, :], in0=ps_o[r][:, :], scalar=rinv[:, r:r + 1],
                                               in1=xres[:, r, :], op0=ALU.mult, op1=ALU.add).then_inc(y_final, 1)

            def layer1(n, r4, queries):
                for q in range(NQ):
                    p_lo(q, B + n * NQ)
                inverse_sum(NT + n, r4 % 2)
                if not (isinstance(n, int) and n == 0):
                    final(n - 1, (r4 + 1) % 2)
                if not (isinstance(n, int) and n == NT - 1):
                    masked1(n + 1)
                if queries is not None:
                    query_lo(queries)

            query_lo(0)
            masked1(0)
            for r in range(4):
                layer1(r, r, 1 if r == 2 else None)
            with dve.Fori(1, NT // 4 - 1, 1) as g:
                for r in range(4):
                    layer1(g * 4 + r, r, g + 1 if r == 2 else None)
            for r in range(4):
                layer1(NT - 4 + r, r, None)
            dve.wait_ge(sum_chain, 3 * 2 * NT)
            final(NT - 1, 1)

        @block.tensor
        def _(pe):
            def product(ps, a_hi, a_lo, b_hi, b_lo, start, stop):
                nc.tensor.matmul(ps, a_hi, b_hi, start=start, stop=False)
                nc.tensor.matmul(ps, a_hi, b_lo, start=False, stop=False)
                return nc.tensor.matmul(ps, a_lo, b_hi, start=False, stop=stop)

            pe.wait_ge(consts, 3)

            def spread(i):
                pe.wait_ge(spread_in, i + 1)
                at_least(pe, spread_used, i)
                nc.tensor.matmul(ps_q[0][:, :], ones, diag, start=True, stop=True).then_inc(spread_out, 1)

            for i in range(3):
                spread(i)

            def values(n, r4, at, last=False):
                r = r4 % 2
                if at == 0:
                    pe.wait_ge(h0_out[r4], (n - r4) * 8 + 32)
                elif last:
                    pe.wait_ge(h1_out, NT * 32)
                else:
                    pe.wait_ge(h_hi_done, at + n + 2)
                at_least(pe, v_lo_done, at + n - 1)
                for c in range(C):
                    k = bass.ds(n * P, P)
                    done = product(ps_o[r][:, :], K_hi[:, c, k], K_lo[:, c, k], W_hi[:, c, :], W_lo[:, c, :],
                                   c == 0, c == C - 1)
                done.then_inc(v_ready, 1)

            pe.wait_ge(w_split, 1)
            for n in range(4):
                values(n, n, 0)
            with pe.Fori(1, NT // 4, 1) as g:
                for r in range(4):
                    values(g * 4 + r, r, 0)
            for g in range(NT // C):
                spread(3 + g)

            def weighted_values(n, r, at):
                for q in range(NQ):
                    pe.wait_ge(pt_in[q], at * 8 + 32)
                    for j in range(q * JQ, (q + 1) * JQ):
                        last = product(ps_o[r][:, :], PT_hi[:, j, :], PT_lo[:, j, :], V_hi[:, j, :], V_lo[:, j, :],
                                       j == 0, j == NT - 1)
                    last.then_inc(pv_done, 1)

            pe.wait_ge(v_lo_done, NT)

            def layer0(n, r):
                at_least(pe, o_relu, n - 1)
                weighted_values(n, r, n * NQ)

            paired_tiles(pe, layer0)

            pe.wait_ge(w_split, 2)
            pe.wait_ge(o_relu, NT - 1)
            values(0, 0, NT)
            pe.wait_ge(o_relu, NT)
            values(1, 1, NT)
            with pe.Fori(1, NT // 2 - 1, 1) as pair:
                for r in range(2):
                    values(pair * 2 + r, r, NT)
            values(NT - 2, 0, NT)
            values(NT - 1, 1, NT, last=True)
            for i in range(2):
                pe.wait_ge(wt_in[i], 8 * 16)
            for d in range(C):
                for c in range(C):
                    k = slice(d * P, (d + 1) * P)
                    last = product(ps_s[d][:, :], sh16[:, 0, 0, c, k], sh16[:, 0, 1, c, k],
                                   sh16[:, 1, 0, c, :], sh16[:, 1, 1, c, :], c == 0, c == C - 1)
                last.then_inc(m_ready, 1)

            def query(g):
                for d in range(C):
                    at_least(pe, q_lo_done, g * C + d - 1)
                    for c in range(C):
                        k = slice(d * P, (d + 1) * P)
                        i = bass.ds(g * D, D)
                        last = product(ps_q[d % 2][:, :], M_hi[:, c, k], M_lo[:, c, k], K_hi[:, c, i], K_lo[:, c, i],
                                       c == 0, c == C - 1)
                    last.then_inc(q_ready, 1)

            def scores(n, r4, g):
                pe.wait_ge(q_lo_done, g * C + C)
                for j in range(NJ):
                    at_least(pe, s_relu, n * NJ + j - 3)
                    i = slice(r4 * P, (r4 + 1) * P)
                    k = slice(j * JB, (j + 1) * JB)
                    for c in range(C):
                        last = product(ps_s[j % 4][:, :], q_hi[:, c, i], q_lo[:, c, i], K_hi[:, c, k], K_lo[:, c, k],
                                       c == 0, c == C - 1)
                    last.then_inc(s_ready, 1)

            pe.wait_ge(m_lo_done, C)
            pe.wait_ge(spread_used, 3 + NT // C)
            query(0)
            pe.wait_ge(v_lo_done, 2 * NT)
            scores(0, 0, 0)

            def layer1(n, r4, g, queries):
                if not (isinstance(n, int) and n == NT - 1):
                    scores(n + 1, (r4 + 1) % 4, g + 1 if r4 == 3 else g)
                if queries is not None:
                    query(queries)
                at_least(pe, y_final, n - 1)
                weighted_values(n, r4 % 2, NT * NQ + n * NQ)

            for r in range(4):
                layer1(r, r, 0, 1 if r == 2 else None)
            with pe.Fori(1, NT // 4 - 1, 1) as g:
                for r in range(4):
                    layer1(g * 4 + r, r, g, g + 1 if r == 2 else None)
            for r in range(4):
                layer1(NT - 4 + r, r, NT // 4 - 1, None)


_INS = ['x', 'adj', 'L0_gnn_W', 'L0_gnn_a1', 'L0_gnn_a2', 'L1_gnn_Wf', 'L1_gnn_bf', 'L1_gnn_Wg', 'L1_gnn_bg',
        'L1_gnn_W', 'L1_gnn_bW']


def kernel(**inputs):
    import numpy as _np
    import concourse.bacc as _bacc
    from concourse import mybir as _mybir
    from concourse.bass_utils import run_bass_kernel_spmd as _run

    nc = _bacc.Bacc("TRN2", target_bir_lowering=False, num_devices=1)
    arrays, args = {}, []
    for name in _INS:
        a = _np.ascontiguousarray(inputs[name])
        arrays[f"in_{name}_dram"] = a
        args.append(nc.dram_tensor(f"in_{name}_dram", a.shape, _mybir.dt.from_np(a.dtype), kind="ExternalInput").ap())
    out = nc.dram_tensor("out_dram", inputs['x'].shape, _mybir.dt.float32, kind="ExternalOutput").ap()
    graph_layers(nc, *args, out)
    r = _run(nc, [arrays], core_ids=[0])
    return r.results[0]["out_dram"]
```

```python
from contextlib import ExitStack

import concourse.bass as bass
from concourse import mybir

F32 = mybir.dt.float32
F16 = mybir.dt.float16
BF16 = mybir.dt.bfloat16
I32 = mybir.dt.int32
ALU = mybir.AluOpType
ACT = mybir.ActivationFunctionType
AX_X = mybir.AxisListType.X

P = 128
SLOPE = 0.2
EPS = 1e-5

H_SCALE = 2.0 ** 10
W_SCALE = 2.0 ** 12
Q_SCALE = 2.0 ** 9
S_SCALE = Q_SCALE * H_SCALE
P_SCALE = 2.0 ** 14
MASK = 9e15 * S_SCALE


def graph_layers(nc, x, adj, W0, a1, a2, Wf, bf, Wg, bg, W1, bW, out):
    N, D = x.shape
    NT = N // P
    C = D // P
    NQ = 4
    QW = N // NQ
    JQ = QW // P
    JB = 512
    NJ = N // JB
    BQ = QW // JB

    x1 = nc.dram_tensor("x1_scratch", [N, D], F32, kind="Internal").ap()

    with ExitStack() as ctx:
        def sb(name, shape, dt):
            return ctx.enter_context(nc.sbuf_tensor(name, shape, dt))

        def sem(name):
            return ctx.enter_context(nc.semaphore(name))

        V_hi = sb("V_hi", [P, NT, D], F16)
        V_lo = sb("V_lo", [P, NT, D], F16)
        K = sb("K", [P, 2, C, N], F16)
        adj_sb = sb("adj_sb", [P, 2, QW], I32)
        mask_sb = sb("mask_sb", [P, 2, QW], BF16)
        score = sb("score", [P, N], F32)
        p_nat = sb("p_nat", [P, 2, 2, QW], F16)
        PT = sb("PT", [P, NQ, 2, JQ, P], F16)
        shared = sb("shared", [P, N], F32)
        xres = sb("xres", [P, 2, D], F32)
        work = sb("work", [P, D], F32)
        h_nat = sb("h_nat", [P, 2, D], F16)
        u_row = sb("u_row", [P, D], F32)
        f12 = sb("f12", [P, NT, 2], F32)
        u = sb("u", [P, NT], F32)
        dots = sb("dots", [P, 1], F32)
        q_bias = sb("q_bias", [P, C], F32)
        vec_col = sb("vec_col", [P, 3, C], F32)
        w12 = sb("w12", [P, 2, C, 2], F16)
        bfbg = sb("bfbg", [P, 1], F32)
        stats = sb("stats", [P, 4, 6], F32)
        mean_var = sb("mean_var", [P, 4, 2], F32)
        ve = sb("ve", [P, 4], F32)
        rstd = sb("rstd", [P, 4], F32)
        shift = sb("shift", [P, 4], F32)
        mhalf = sb("mhalf", [P, 4], F32)
        ones4 = sb("ones4", [P, NQ], F32)
        mask_bias = sb("mask_bias", [P, 1], F32)
        qmax = sb("qmax", [P, NQ], F32)
        rowmax = sb("rowmax", [P, 2], F32)
        neg_max = sb("neg_max", [P, 1], F32)
        qsum = sb("qsum", [P, NQ], F32)
        qweighed = sb("qweighed", [P, NQ], F32)
        rowsum = sb("rowsum", [P, 1], F32)
        rinv = sb("rinv", [P, 2], F32)

        def f32_rows(region):
            return region.bitcast(F32).rearrange("p (c n) -> p c n", n=D)

        K_hi, K_lo = K[:, 0], K[:, 1]
        K_blocks = K[:, :, :, :].rearrange("p s c n -> p (s c) n")
        pt_flat = PT[:, :, :, :, :].rearrange("p q s j i -> p (q s j i)")
        w_f32 = score[:, 0:C * D].rearrange("p (c n) -> p c n", c=C)
        W0_16 = pt_flat[:, 2 * C * D:4 * C * D].rearrange("p (s c n) -> p s c n", s=2, c=C)
        W1_16 = score[:, C * D:2 * C * D].bitcast(F16).rearrange("p (s c n) -> p s c n", s=2, c=C)
        vecs = f32_rows(adj_sb[:, :, :].rearrange("p a b -> p (a b)"))
        v_tail = [V[:, NT // 2:NT, :].rearrange("p a b -> p (a b)") for V in (V_hi, V_lo)]
        wf_nat = f32_rows(v_tail[0][:, 0:2 * C * D])
        wg_nat = f32_rows(v_tail[0][:, 2 * C * D:4 * C * D])
        xin = [f32_rows(pt_flat[:, 0:2 * C * D]), f32_rows(v_tail[1][:, 2 * C * D:4 * C * D])]
        pn32 = p_nat[:, :, :, :].rearrange("p a b c -> p (a b c)").bitcast(F32)
        diag = pn32[:, 0:D]
        junk = pn32[:, D:2 * D]
        ident = pn32[:, 2 * D:2 * D + P]
        ones = pn32[:, 2 * D + P:2 * D + 2 * P]
        h_f32 = [work[:, :], xres[:, 0, :]]
        h_halves = [h_nat[:, :, :], xres[:, 1, :].bitcast(F16).rearrange("p (s n) -> p s n", s=2)]
        wl = [f32_rows(pt_flat[:, i * 2 * C * D:(i + 1) * 2 * C * D]) for i in range(2)]
        ws = p_nat[:, :, :, :].rearrange("p a b (c n) -> p a (b c) n", n=D)
        sh16 = shared[:, :].bitcast(F16).rearrange("p (m s c n) -> p m s c n", m=2, s=2, c=C)
        M_hi, M_lo = sh16[:, 0, 0], sh16[:, 0, 1]
        q_hi, q_lo = sh16[:, 1, 0], sh16[:, 1, 1]

        ps_o = [ctx.enter_context(nc.psum_tensor(f"ps_o{i}", [P, D], F32)) for i in range(2)]
        ps_q = [ctx.enter_context(nc.psum_tensor(f"ps_q{i}", [P, D], F32)) for i in range(2)]
        ps_v = [ps_o[0], ps_o[1], ps_q[0]]
        ps_s = [ctx.enter_context(nc.psum_tensor(f"ps_s{i}", [P, JB], F32)) for i in range(4)]

        V1_M, V1_Q = 18, 24
        ps_f, ps_row = ps_s[0], ps_s[1]

        VG = 3
        NG = NT // 4
        V_TAIL = VG * (NG - 1)

        w0_in = sem("w0_in")
        params_in = sem("params_in")
        x_in = [sem(f"x_in{i}") for i in range(8)]
        xres_in = [sem(f"xres_in{i}") for i in range(2)]
        adj_in = [sem(f"adj_in{i}") for i in range(2)]
        h0_out = [sem(f"h0_out{i}") for i in range(8)]
        h1_out = sem("h1_out")
        pt_in = [sem(f"pt_in{q}") for q in range(NQ)]
        x1_out = [sem(f"x1_out{i}") for i in range(2)]
        y_out = [sem(f"y_out{i}") for i in range(2)]
        w1_in = sem("w1_in")
        wfg_in = sem("wfg_in")
        wt_in = [sem(f"wt_in{i}") for i in range(2)]
        stood = sem("stood")
        consts = sem("consts")
        zeroed = sem("zeroed")
        tick = sem("tick")
        w_split = sem("w_split")
        w_hi_done = sem("w_hi_done")
        spread_in = sem("spread_in")
        spread_out = sem("spread_out")
        spread_used = sem("spread_used")
        bn_done = sem("bn_done")
        aggr_done = sem("aggr_done")
        ve_done = sem("ve_done")
        rstd_done = sem("rstd_done")
        shift_done = sem("shift_done")
        h_done = sem("h_done")
        h_hi_done = sem("h_hi_done")
        h_lo_done = sem("h_lo_done")
        h_used = sem("h_used")
        u_done = sem("u_done")
        vectors_done = sem("vectors_done")
        w12_hi = sem("w12_hi")
        w12_done = sem("w12_done")
        f_ready = sem("f_ready")
        f_done = sem("f_done")
        v_ready = sem("v_ready")
        v_biased = sem("v_biased")
        v_hi_done = sem("v_hi_done")
        v_lo_done = sem("v_lo_done")
        mask_done = sem("mask_done")
        z_done = sem("z_done")
        max_chain = sem("max_chain")
        y0_done = sem("y0_done")
        y_done = sem("y_done")
        leaky_done = sem("leaky_done")
        exp_done = sem("exp_done")
        p_hi_done = sem("p_hi_done")
        p_lo_done = sem("p_lo_done")
        sum_chain = sem("sum_chain")
        pv_done = sem("pv_done")
        o_relu = sem("o_relu")
        x1_done = sem("x1_done")
        y_final = sem("y_final")
        m_ready = sem("m_ready")
        m_hi_done = sem("m_hi_done")
        m_lo_done = sem("m_lo_done")
        q_ready = sem("q_ready")
        q_biased = sem("q_biased")
        q_hi_done = sem("q_hi_done")
        q_lo_done = sem("q_lo_done")
        s_ready = sem("s_ready")
        s_relu = sem("s_relu")

        def at_least(eng, semaphore, value):
            if not isinstance(value, int) or value > 0:
                eng.wait_ge(semaphore, value)

        def query_bank(g, c):
            return (ps_s[c] if isinstance(g, int) and g == 0 else ps_q[c % 2])[:, :]

        def until(eng, semaphore, value):
            if isinstance(value, int):
                at_least(eng, semaphore, value)
            else:
                eng.wait_ge(semaphore, value).then_inc(stood, 1)

        def in_threes(eng, lo, hi, body):
            with eng.Fori(lo // 3, hi // 3, 1) as three:
                for k in range(3):
                    body(three * 3 + k, k)

        def grouped_tiles(eng, body):
            body(0, 0)
            body(1, 1)
            with eng.Fori(1, NG // 2, 1) as pair:
                for r in range(2):
                    body(pair * 2 + r, r)

        def paired_tiles(eng, body):
            body(0, 0)
            body(1, 1)
            with eng.Fori(1, NT // 2 - 1, 1) as pair:
                for r in range(2):
                    body(pair * 2 + r, r)
            body(NT - 2, 0)
            body(NT - 1, 1)

        def rows(t, n):
            return t[bass.ds(n * P, P), :]

        block = ctx.enter_context(nc.Block())

        @block.sync
        def _(sp):
            def broadcast(v):
                return v.rearrange("(a n) -> a n", a=1).broadcast_to([P, D])

            def load_x(n, r4, g2):
                sp.dma_start(xin[g2][:, r4, :], rows(x, n)).then_inc(x_in[4 * g2 + r4], 16)

            for n in range(4):
                load_x(n, n, 0)
            sp.dma_start(w_f32, W0.rearrange("(c p) n -> p c n", p=P)).then_inc(w0_in, 16)
            for i, v in enumerate((a1, a2)):
                sp.dma_start(vecs[:, i, :], broadcast(v.rearrange("a b -> (a b)"))).then_inc(w0_in, 16)
            for n in range(4):
                load_x(n + 4, n, 1)
            for i, v in enumerate((bf, bg)):
                sp.dma_start(vecs[:, 2 + i, :], broadcast(v)).then_inc(params_in, 16)
            sp.dma_start(wf_nat, Wf.rearrange("(c p) n -> p c n", p=P)).then_inc(params_in, 16)
            sp.dma_start(wg_nat, Wg.rearrange("(c p) n -> p c n", p=P)).then_inc(params_in, 16)

            def group0(g, g2):
                for r in range(4):
                    n = g * 4 + r
                    until(sp, h_hi_done, n + 1)
                    until(sp, h_lo_done, n + 1)
                    if r == 0:
                        until(sp, f_ready, g - 1)
                    sp.dma_start_transpose(K_blocks[:, :, bass.ds(n * P, P)],
                                           h_halves[r % 2].rearrange("p s n -> p (s n)")).then_inc(h0_out[4 * g2 + r], 16)

            def group0_and_x(g, g2):
                group0(g, g2)
                for r in range(4):
                    load_x(g * 4 + (r + 8), r, g2)

            group0_and_x(0, 0)
            group0_and_x(1, 1)
            with sp.Fori(1, NG // 2 - 1, 1) as pair:
                for r in range(2):
                    group0_and_x(pair * 2 + r, r)
            group0(NG - 2, 0)
            group0(NG - 1, 1)

            sp.wait_ge(vectors_done, 1)

            def load_adj(n, q, at):
                until(sp, mask_done, at + q - 1)
                sp.dma_start(adj_sb[:, q % 2, :], adj[bass.ds(n * P, P), q * QW:(q + 1) * QW]).then_inc(adj_in[q % 2], 16)

            def transpose_p(q, at):
                until(sp, p_lo_done, at + q + 1)
                until(sp, pv_done, at - NQ + q + 1)
                sp.dma_start_transpose(PT[:, q].rearrange("p s j i -> p (s j) i"),
                                       p_nat[:, q % 2].rearrange("p s n -> p (s n)")).then_inc(pt_in[q], 16)

            def store_x1(n, r):
                until(sp, x1_done, n + 1)
                sp.dma_start(rows(x1, n), xres[:, r, :]).then_inc(x1_out[r], 16)

            def load_xres(n, r, stored):
                if stored is not None:
                    sp.wait_ge(x1_out[r], stored)
                    until(sp, h_done, NT + n - 1)
                sp.dma_start(xres[:, r, :], rows(x, n)).then_inc(xres_in[r], 16)

            def transpose_h1(n):
                until(sp, h_hi_done, NT + n + 1)
                until(sp, h_lo_done, NT + n + 1)
                sp.dma_start_transpose(K_blocks[:, :, bass.ds(n * P, P)],
                                       h_nat[:, :, :].rearrange("p s n -> p (s n)")).then_inc(h1_out, 16)

            load_adj(0, 0, 0)
            load_adj(0, 1, 0)
            load_adj(0, 2, 0)
            load_adj(0, 3, 0)
            load_adj(1, 0, NQ)
            load_adj(1, 1, NQ)
            for r in range(4):
                sp.wait_ge(h0_out[4 + r], NG // 2 * 16)
            load_xres(0, 0, None)
            load_xres(1, 1, None)

            def layer0(n, r):
                early = isinstance(n, int) and n < 2
                last = isinstance(n, int) and n == NT - 1
                transpose_p(0, n * NQ)
                if not last:
                    load_adj(n + 1, 2, n * NQ + NQ)
                transpose_p(1, n * NQ)
                if not last:
                    load_adj(n + 1, 3, n * NQ + NQ)
                if not early:
                    store_x1(n - 2, r)
                    transpose_h1(n - 2)
                if isinstance(n, int) and n == 0:
                    sp.wait_ge(v_ready, NT)
                transpose_p(2, n * NQ)
                if not (isinstance(n, int) and n >= NT - 2):
                    load_adj(n + 2, 0, n * NQ + 2 * NQ)
                transpose_p(3, n * NQ)
                if not (isinstance(n, int) and n >= NT - 2):
                    load_adj(n + 2, 1, n * NQ + 2 * NQ)
                if not early:
                    load_xres(n, r, (n - r) * 8)

            paired_tiles(sp, layer0)

            sp.wait_ge(p_lo_done, NT * NQ)
            sp.dma_start(w_f32, W1.rearrange("(c p) n -> p c n", p=P)).then_inc(w1_in, 16)
            sp.wait_ge(mask_done, NT * NQ)
            sp.dma_start(vecs[:, 2, :], bW.rearrange("(a n) -> a n", a=1).broadcast_to([P, D])).then_inc(w1_in, 16)
            for n in range(NT - 2, NT):
                store_x1(n, n % 2)
                transpose_h1(n)
            sp.wait_ge(pv_done, NT * NQ)
            for i, w in enumerate((Wf, Wg)):
                sp.dma_start(wl[i], w.rearrange("(c p) n -> p c n", p=P)).then_inc(wfg_in, 16)
            for i in range(2):
                sp.wait_ge(w_split, 2 + i + 1)
                for half in range(2):
                    for c in range(C):
                        sp.dma_start_transpose(sh16[:, i, half, :, c * P:(c + 1) * P],
                                               ws[:, half, c, :]).then_inc(wt_in[i], 16)

            B = NT * NQ
            sp.wait_ge(v_biased, NT)
            for q in range(2):
                sp.dma_start(adj_sb[:, q, :], adj[0:P, q * QW:(q + 1) * QW]).then_inc(adj_in[q], 16)
            load_adj(0, 2, B)
            load_adj(0, 3, B)
            load_adj(1, 0, B + NQ)
            load_adj(1, 1, B + NQ)
            for r in range(2):
                sp.wait_ge(x1_out[r], NT // 2 * 16)
                sp.wait_ge(h_done, 2 * NT)
                sp.dma_start(xres[:, r, :], x1[r * P:(r + 1) * P, :]).then_inc(xres_in[r], 16)

            def layer1(n, r):
                for q in range(NQ):
                    transpose_p(q, B + n * NQ)
                if not (isinstance(n, int) and n == NT - 1):
                    load_adj(n + 1, 2, B + n * NQ + NQ)
                    load_adj(n + 1, 3, B + n * NQ + NQ)
                if not (isinstance(n, int) and n == 0):
                    m, s = n - 1, 1 - r
                    until(sp, y_final, n)
                    sp.dma_start(rows(out, m), xres[:, s, :]).then_inc(y_out[s], 16)
                if not (isinstance(n, int) and n >= NT - 2):
                    load_adj(n + 2, 0, B + n * NQ + 2 * NQ)
                    load_adj(n + 2, 1, B + n * NQ + 2 * NQ)
                if not (isinstance(n, int) and (n == 0 or n == NT - 1)):
                    m, s = n - 1, 1 - r
                    sp.wait_ge(y_out[s], (m - s) * 8 + 16)
                    sp.dma_start(xres[:, s, :], rows(x1, n + 1)).then_inc(xres_in[s], 16)

            paired_tiles(sp, layer1)
            sp.wait_ge(y_final, NT)
            sp.dma_start(rows(out, NT - 1), xres[:, 1, :]).then_inc(y_out[1], 16)
            for r in range(2):
                sp.wait_ge(y_out[r], NT // 2 * 16)

        @block.gpsimd
        def _(pool):
            nc.gpsimd.memset(ident, 0.0).then_inc(zeroed, 1)
            nc.gpsimd.memset(ones, 1.0).then_inc(consts, 1)
            nc.gpsimd.memset(mhalf[:, :], -0.5).then_inc(zeroed, 1)
            nc.gpsimd.memset(ones4[:, :], 1.0).then_inc(consts, 1)
            nc.gpsimd.memset(mask_bias[:, :], MASK).then_inc(consts, 1)
            pool.wait_ge(zeroed, 2)
            nc.gpsimd.affine_select(out=ident, in_=ident, compare_op=ALU.not_equal, fill=1.0, base=0,
                                    pattern=[[-1, P]], channel_multiplier=1).then_inc(consts, 1)
            def inverse_deviation(k, tiles, used):
                s = slice(0, tiles)
                until(pool, aggr_done, k + 1)
                nc.gpsimd.tensor_scalar(ve[:, s], mean_var[:, s, 1], EPS, H_SCALE ** -2,
                                        ALU.add, ALU.mult).then_inc(ve_done, 1)
                pool.wait_ge(ve_done, k + 1)
                at_least(pool, h_done, used)
                nc.gpsimd.tensor_tensor(rstd[:, s], ve[:, s], mhalf[:, s], ALU.pow).then_inc(rstd_done, 1)

            inverse_deviation(0, 4, 0)
            with pool.Fori(1, NG, 1) as g:
                inverse_deviation(g, 4, g * 4)
            with pool.Fori(0, NT, 1) as n:
                inverse_deviation(n + NG, 1, n + NT)

        @block.scalar
        def _(act):
            def split_hi(w, hi, loaded, value, done):
                act.wait_ge(loaded, value)
                nc.scalar.mul(hi, w, W_SCALE).then_inc(done, 1)

            split_hi(w_f32, W0_16[:, 0], w0_in, 3 * 16, w_hi_done)

            def value_hi(n, k):
                act.wait_ge(v_ready, n + 1)
                nc.scalar.activation(V_hi[:, bass.ds(n, 1), :], ps_v[k][:, :].rearrange("p (a n) -> p a n", a=1),
                                     ACT.Copy, scale=1.0 / W_SCALE).then_inc(v_hi_done, 1)

            def group0(g, g2):
                first = isinstance(g, int) and g == 0

                def relu_h(r):
                    n = g * 4 + r
                    if r == 0:
                        act.wait_ge(shift_done, g + 1)
                    at_least(act, h_lo_done, n - 1)
                    nc.scalar.activation(h_f32[r % 2], xin[g2][:, r, :], ACT.Relu, bias=shift[:, r:r + 1],
                                         scale=rstd[:, r:r + 1]).then_inc(h_done, 1)

                def high_half(r):
                    act.wait_ge(h_done, g * 4 + (r + 1))
                    if r >= 2:
                        act.wait_ge(h0_out[4 * g2 + r - 2], (g - g2) * 8 + 16)
                    elif not first:
                        act.wait_ge(h0_out[4 * (1 - g2) + r + 2], (g - g2) * 8 + 16 * g2)
                    nc.scalar.copy(h_halves[r % 2][:, 0, :], h_f32[r % 2]).then_inc(h_hi_done, 1)

                relu_h(0)
                relu_h(1)
                high_half(0)
                high_half(1)
                if not first:
                    value_hi((g - 1) * VG, 0)
                relu_h(2)
                relu_h(3)
                high_half(2)
                high_half(3)
                if not first:
                    value_hi((g - 1) * VG + 1, 1)
                    value_hi((g - 1) * VG + 2, 2)

            grouped_tiles(act, group0)

            def mask(q, at):
                act.wait_ge(adj_in[q % 2], at * 8 + 16 * (q // 2 + 1))
                at_least(act, z_done, at + q - 1)
                nc.scalar.activation(mask_sb[:, q % 2, :], adj_sb[:, q % 2, :], ACT.Relu,
                                     bias=mask_bias[:, :], scale=-MASK).then_inc(mask_done, 1)

            def exp_quarter(q, at, scale):
                nc.scalar.activation(score[:, q * QW:(q + 1) * QW], score[:, q * QW:(q + 1) * QW], ACT.Exp,
                                     bias=neg_max[:, :], scale=scale,
                                     accum_out=qsum[:, q:q + 1]).then_inc(exp_done, 1)

            def p_hi(q, at):
                act.wait_ge(exp_done, at + q + 1)
                if q >= 2:
                    act.wait_ge(pt_in[q - 2], at * 4 + 16)
                else:
                    at_least(act, pt_in[q + 2], at * 4)
                nc.scalar.mul(p_nat[:, q % 2, 0, :], score[:, q * QW:(q + 1) * QW], P_SCALE).then_inc(p_hi_done, 1)

            def add_f1(n, q):
                s = slice(q * QW, (q + 1) * QW)
                until(act, z_done, n * NQ + q + 1)
                nc.scalar.activation(score[:, s], score[:, s], ACT.Identity,
                                     bias=f12[:, bass.ds(n, 1), 0]).then_inc(y_done, 1)

            def relu_out(n, r):
                act.wait_ge(pv_done, n * NQ + NQ)
                act.wait_ge(sum_chain, 2 * n + 2)
                at_least(act, h_used, n)
                nc.scalar.activation(work[:, :], ps_o[r][:, :], ACT.Relu, scale=rinv[:, r:r + 1]).then_inc(o_relu, 1)

            def norm1(n, r):
                act.wait_ge(shift_done, NG + n + 1)
                nc.scalar.activation(work[:, :], xres[:, r, :], ACT.Relu, bias=shift[:, 0:1],
                                     scale=rstd[:, 0:1]).then_inc(h_done, 1)
                act.wait_ge(h_done, NT + n + 1)
                at_least(act, h1_out, n * 16)
                nc.scalar.copy(h_nat[:, 0, :], work[:, :]).then_inc(h_hi_done, 1)

            tail = iter(range(V_TAIL, NT))

            def spare(count=1):
                for _, v in zip(range(count), tail):
                    value_hi(v, v % 3)

            def layer0(n, r):
                first = isinstance(n, int) and n == 0
                early = isinstance(n, int) and n < 2
                last = isinstance(n, int) and n == NT - 1
                at = n * NQ
                if not early:
                    relu_out(n - 2, r)
                if first:
                    act.wait_ge(spread_used, 1 + NG)
                at_least(act, sum_chain, 2 * n - 1)
                act.wait_ge(max_chain, 3 * n + 3)
                for q in range(2):
                    act.wait_ge(leaky_done, at + q + 1)
                    exp_quarter(q, at, 1.0)
                p_hi(0, at)
                if not last:
                    mask(0, at + NQ)
                if first:
                    spare()
                act.wait_ge(leaky_done, at + 3)
                exp_quarter(2, at, 1.0)
                p_hi(1, at)
                if not last:
                    mask(1, at + NQ)
                if first:
                    spare()
                act.wait_ge(leaky_done, at + 4)
                exp_quarter(3, at, 1.0)
                p_hi(2, at)
                if first:
                    spare()
                if not early:
                    norm1(n - 2, r)
                if not last:
                    mask(2, at + NQ)
                p_hi(3, at)
                if first:
                    spare()
                if not last:
                    add_f1(n + 1, 1)
                    mask(3, at + NQ)
                    add_f1(n + 1, 2)
                    add_f1(n + 1, 3)
                if first:
                    spare(NT)

            mask(0, 0)
            mask(1, 0)
            spare(2)
            mask(2, 0)
            spare()
            add_f1(0, 1)
            mask(3, 0)
            spare()
            add_f1(0, 2)
            add_f1(0, 3)
            spare()
            paired_tiles(act, layer0)

            split_hi(w_f32, W1_16[:, 0], w1_in, 2 * 16, w_hi_done)
            for n in range(NT - 2, NT):
                relu_out(n, n % 2)
                norm1(n, n % 2)

            def value_hi1(n, k):
                act.wait_ge(v_biased, n + 1)
                nc.scalar.copy(V_hi[:, bass.ds(n, 1), :],
                               ps_v[k][:, :].rearrange("p (a n) -> p a n", a=1)).then_inc(v_hi_done, 1)

            def weight_hi(i):
                act.wait_ge(wfg_in, 2 * 16)
                if i:
                    act.wait_ge(wt_in[0], 8 * 16)
                nc.scalar.mul(ws[:, 0], wl[i], W_SCALE).then_inc(w_hi_done, 1)

            def query_hi(g):
                for c in range(C):
                    act.wait_ge(q_biased, g * C + c + 1)
                    nc.scalar.copy(q_hi[:, c, :], query_bank(g, c)).then_inc(q_hi_done, 1)

            B = NT * NQ

            def relu_scores(n):
                at = B + n * NQ
                for q in range(NQ):
                    mask(q, at)
                    act.wait_ge(p_lo_done, at - NQ + q + 1)
                    for b in range(BQ):
                        j = q * BQ + b
                        until(act, s_ready, n * NJ + j + 1)
                        nc.scalar.activation(score[:, j * JB:(j + 1) * JB], ps_s[j % 4][:, :], ACT.Relu,
                                             bias=u[:, bass.ds(n, 1)]).then_inc(s_relu, 1)

            def layer1(n, r4, queries):
                at = B + n * NQ
                act.wait_ge(sum_chain, 2 * NT + 2 * n)
                act.wait_ge(max_chain, 3 * NT + 2 * n + 2)
                for q in range(2):
                    exp_quarter(q, at, 1.0 / S_SCALE)
                p_hi(0, at)
                for q in range(2, NQ):
                    exp_quarter(q, at, 1.0 / S_SCALE)
                    p_hi(q - 1, at)
                p_hi(3, at)
                if not (isinstance(n, int) and n == NT - 1):
                    relu_scores(n + 1)
                if queries is not None:
                    query_hi(queries)

            in_threes(act, 0, 6, value_hi1)
            weight_hi(0)
            in_threes(act, 6, 12, value_hi1)
            weight_hi(1)
            in_threes(act, 12, V1_M, value_hi1)
            act.wait_ge(m_ready, C)
            for c in range(C):
                nc.scalar.activation(M_hi[:, c, :], ps_s[c][:, :], ACT.Copy, scale=1.0 / W_SCALE).then_inc(m_hi_done, 1)
            in_threes(act, V1_M, V1_Q, value_hi1)
            query_hi(0)
            in_threes(act, V1_Q, NT - 2, value_hi1)
            value_hi1(NT - 2, 0)
            value_hi1(NT - 1, 1)
            act.wait_ge(u_done, NT + 1)
            relu_scores(0)
            with act.Fori(0, NT // 4 - 1, 1) as g:
                for r in range(4):
                    layer1(g * 4 + r, r, g + 1 if r == 2 else None)
            for r in range(4):
                layer1(NT - 4 + r, r, None)

        @block.vector
        def _(dve):
            ticks = [0]

            def ticked(ins):
                ins.then_inc(tick, 1)
                ticks[0] += 1
                return ticks[0]

            def split_lo(w, hi, lo):
                return nc.vector.scalar_tensor_tensor(out=lo, in0=w, scalar=W_SCALE, in1=hi,
                                                      op0=ALU.mult, op1=ALU.subtract)

            def dot(o, a, b, scale, acc):
                return nc.vector.tensor_tensor_reduce(out=o, in0=a, in1=b, scale=scale, scalar=0.0,
                                                      op0=ALU.mult, op1=ALU.add, accum_out=acc)

            def rank_one(pairs):
                t = ticks[0]
                for w, vec, scale, acc in pairs:
                    at_least(dve, tick, t)
                    t = ticked(dot(junk, w, vecs[:, vec, :], scale, acc))
                dve.wait_ge(tick, t)

            def spread_start(col):
                for c in range(C):
                    last = nc.vector.tensor_scalar(diag[:, c * P:(c + 1) * P], ident, col(c), None, ALU.mult)
                last.then_inc(spread_in, 1)

            def spread_end(i, dst):
                until(dve, spread_out, i + 1)
                nc.vector.tensor_copy(dst, ps_row[:, :]).then_inc(spread_used, 1)

            def statistics(xt, k, tiles):
                for r in range(tiles):
                    if tiles > 1:
                        x_arrived(k, r)
                    nc.vector.bn_stats(stats[:, r, :], xt(r)).then_inc(bn_done, 1)
                for r in range(tiles):
                    if r == 0:
                        dve.wait_ge(bn_done, k * 4 + 4 if tiles > 1 else k + (4 * NG - NG + 1))
                        until(dve, rstd_done, k)
                    last = nc.vector.bn_aggr(mean_var[:, r, :], stats[:, r, :])
                last.then_inc(aggr_done, 1)

            def make_shift(k, tiles):
                s = slice(0, tiles)
                dve.wait_ge(rstd_done, k + 1)
                nc.vector.scalar_tensor_tensor(out=shift[:, s], in0=mean_var[:, s, 0], scalar=-1.0,
                                               in1=rstd[:, s], op0=ALU.mult, op1=ALU.mult).then_inc(shift_done, 1)

            def value_lo(n, k, scale=1.0 / W_SCALE, at=0):
                dve.wait_ge(v_hi_done, at + n + 1)
                nc.vector.scalar_tensor_tensor(out=V_lo[:, bass.ds(n, 1), :],
                                               in0=ps_v[k][:, :].rearrange("p (a n) -> p a n", a=1), scalar=scale,
                                               in1=V_hi[:, bass.ds(n, 1), :],
                                               op0=ALU.mult, op1=ALU.subtract).then_inc(v_lo_done, 1)

            def take_f(g):
                dve.wait_ge(f_ready, g + 1)
                nc.vector.tensor_scalar(f12[:, bass.ds(g * 4, 4), :],
                                        ps_f[:, 0:8].rearrange("p (t v) -> p t v", v=2),
                                        1.0 / (H_SCALE * W_SCALE), None, ALU.mult).then_inc(f_done, 1)

            def spread_f(g):
                dve.wait_ge(f_done, g + 1)
                spread_start(lambda c: f12[:, bass.ds(g * 4 + c, 1), 1])

            def spread_f_end(g):
                spread_end(g + 1, shared[:, bass.ds(g * D, D)])

            def x_arrived(g, r):
                g2 = group_parity[0]
                dve.wait_ge(x_in[4 * g2 + r], (g - g2) * 8 + 16)

            group_parity = [0]

            def group0(g, g2):
                first = isinstance(g, int) and g == 0
                second = isinstance(g, int) and g == 1
                group_parity[0] = g2
                statistics(lambda r: xin[g2][:, r, :], g, 4)
                if not first:
                    take_f(g - 1)
                    if not second:
                        spread_f_end(g - 2)
                    spread_f(g - 1)
                make_shift(g, 4)

                def low_half(r):
                    dve.wait_ge(h_hi_done, g * 4 + (r + 1))
                    nc.vector.tensor_tensor(h_halves[r % 2][:, 1, :], h_f32[r % 2], h_halves[r % 2][:, 0, :],
                                            ALU.subtract).then_inc(h_lo_done, 1)

                low_half(0)
                low_half(1)
                if not first:
                    value_lo((g - 1) * VG, 0)
                low_half(2)
                low_half(3)
                if not first:
                    value_lo((g - 1) * VG + 1, 1)
                    value_lo((g - 1) * VG + 2, 2)
                if first:
                    vectors()

            def vectors():
                dve.wait_ge(w0_in, 3 * 16)
                dve.wait_ge(w_hi_done, 1)
                split_lo(w_f32, W0_16[:, 0], W0_16[:, 1]).then_inc(w_split, 1)
                rank_one([(w_f32[:, c, :], v, W_SCALE, vec_col[:, v, c:c + 1]) for v in range(2) for c in range(C)])
                nc.vector.tensor_copy(w12[:, 0], vec_col[:, 0:2, :].rearrange("p v c -> p c v")).then_inc(w12_hi, 1)
                dve.wait_ge(w12_hi, 1)
                nc.vector.tensor_tensor(w12[:, 1], vec_col[:, 0:2, :].rearrange("p v c -> p c v"), w12[:, 0],
                                        ALU.subtract).then_inc(w12_done, 1)
                dve.wait_ge(params_in, 4 * 16)
                rank_one([(wf_nat[:, c, :], 3, 1.0, vec_col[:, 2, c:c + 1]) for c in range(C)]
                         + [(wg_nat[:, c, :], 2, Q_SCALE, q_bias[:, c:c + 1]) for c in range(C)]
                         + [(vecs[:, 2, :], 3, S_SCALE, bfbg[:, :])])
                dve.wait_ge(consts, 4)
                spread_start(lambda c: vec_col[:, 2, c:c + 1])
                spread_end(0, u_row[:, :])
                dve.wait_ge(spread_used, 1)
                nc.vector.memset(dots[:, :], 0.0).then_inc(vectors_done, 1)

            grouped_tiles(dve, group0)
            take_f(NG - 1)
            spread_f_end(NG - 2)
            spread_f(NG - 1)

            def masked(q, at):
                at_least(dve, p_lo_done, at - NQ + q + 1)
                until(dve, mask_done, at + q + 1)
                s = slice(q * QW, (q + 1) * QW)
                nc.vector.tensor_tensor_reduce(out=score[:, s], in0=shared[:, s], in1=mask_sb[:, q % 2, :], scale=1.0,
                                               scalar=-3e38, op0=ALU.subtract, op1=ALU.max,
                                               accum_out=qmax[:, q:q + 1]).then_inc(z_done, 1)

            def quarters_max():
                return nc.vector.reduce_max(rowmax[:, 0:1], qmax[:, :], AX_X)

            def add_f1(n):
                dve.wait_ge(z_done, n * NQ + 1)
                nc.vector.tensor_scalar(score[:, 0:QW], score[:, 0:QW], f12[:, bass.ds(n, 1), 0], None,
                                        ALU.add).then_inc(y0_done, 1)

            def leaky(n, q):
                s = slice(q * QW, (q + 1) * QW)
                if q == 0:
                    dve.wait_ge(y0_done, n + 1)
                else:
                    dve.wait_ge(y_done, n * (NQ - 1) + q)
                nc.vector.scalar_tensor_tensor(out=score[:, s], in0=score[:, s], scalar=SLOPE, in1=score[:, s],
                                               op0=ALU.mult, op1=ALU.max).then_inc(leaky_done, 1)

            def p_lo(q, at):
                dve.wait_ge(p_hi_done, at + q + 1)
                nc.vector.scalar_tensor_tensor(out=p_nat[:, q % 2, 1, :], in0=score[:, q * QW:(q + 1) * QW],
                                               scalar=P_SCALE, in1=p_nat[:, q % 2, 0, :],
                                               op0=ALU.mult, op1=ALU.subtract).then_inc(p_lo_done, 1)

            def row_sum(n):
                dve.wait_ge(exp_done, n * NQ + NQ)
                nc.vector.tensor_tensor_reduce(out=qweighed[:, :], in0=qsum[:, :], in1=ones4[:, :],
                                               scale=P_SCALE * H_SCALE, scalar=0.0, op0=ALU.mult, op1=ALU.add,
                                               accum_out=rowsum[:, :]).then_inc(sum_chain, 1)

            def inverse_sum(n, r):
                dve.wait_ge(sum_chain, 2 * n + 1)
                nc.vector.reciprocal(rinv[:, r:r + 1], rowsum[:, :]).then_inc(sum_chain, 1)

            def residual0(n, r):
                dve.wait_ge(o_relu, n + 1)
                dve.wait_ge(xres_in[r], (n - r) * 8 + 16)
                nc.vector.tensor_tensor(xres[:, r, :], xres[:, r, :], work[:, :], ALU.add).then_inc(x1_done, 1)
                dve.wait_ge(x1_done, n + 1)
                statistics(lambda _: xres[:, r, :], NG + n, 1)

            def products1(n):
                dve.wait_ge(h_hi_done, NT + n + 1)
                nc.vector.tensor_tensor(h_nat[:, 1, :], work[:, :], h_nat[:, 0, :], ALU.subtract).then_inc(h_lo_done, 1)
                dve.wait_ge(h_lo_done, NT + n + 1)
                dot(work[:, :], work[:, :], u_row[:, :], S_SCALE / H_SCALE, dots[:, :]).then_inc(h_used, 1)
                dve.wait_ge(h_used, n + 1)
                nc.vector.tensor_copy(u[:, bass.ds(n, 1)], dots[:, :]).then_inc(u_done, 1)

            tail = iter(range(V_TAIL, NT))

            def spare(count=1):
                for _, v in zip(range(count), tail):
                    value_lo(v, v % 3)

            def layer0(n, r):
                first = isinstance(n, int) and n == 0
                early = isinstance(n, int) and n < 2
                last = isinstance(n, int) and n == NT - 1
                at = n * NQ
                if not first:
                    row_sum(n - 1)
                dve.wait_ge(z_done, at + NQ)
                quarters_max().then_inc(max_chain, 1)
                add_f1(n)
                dve.wait_ge(max_chain, 3 * n + 1)
                nc.vector.tensor_scalar(rowmax[:, 1:2], rowmax[:, 0:1], f12[:, bass.ds(n, 1), 0], -1.0,
                                        ALU.add, ALU.mult).then_inc(max_chain, 1)
                leaky(n, 0)
                dve.wait_ge(max_chain, 3 * n + 2)
                nc.vector.scalar_tensor_tensor(out=neg_max[:, :], in0=rowmax[:, 1:2], scalar=SLOPE,
                                               in1=rowmax[:, 1:2], op0=ALU.mult, op1=ALU.min).then_inc(max_chain, 1)
                if not first:
                    inverse_sum(n - 1, 1 - r)
                else:
                    spare()
                leaky(n, 1)
                leaky(n, 2)
                leaky(n, 3)
                if first:
                    spare()
                if not early:
                    residual0(n - 2, r)
                p_lo(0, at)
                if not early:
                    make_shift(NG + n - 2, 1)
                p_lo(1, at)
                if first:
                    spare()
                if not last:
                    masked(0, at + NQ)
                p_lo(2, at)
                if first:
                    spare()
                if not last:
                    masked(1, at + NQ)
                if not early:
                    products1(n - 2)
                p_lo(3, at)
                if first:
                    spare()
                if not last:
                    masked(2, at + NQ)
                    masked(3, at + NQ)
                if first:
                    spare(NT)

            spare()
            spread_f_end(NG - 1)
            dve.wait_ge(spread_used, 1 + NG)
            masked(0, 0)
            masked(1, 0)
            spare(2)
            masked(2, 0)
            masked(3, 0)
            spare()

            paired_tiles(dve, layer0)

            row_sum(NT - 1)
            inverse_sum(NT - 1, 1)

            dve.wait_ge(w1_in, 2 * 16)
            dve.wait_ge(w_hi_done, 2)
            split_lo(w_f32, W1_16[:, 0], W1_16[:, 1]).then_inc(w_split, 1)
            t = ticked(nc.vector.tensor_scalar(vecs[:, 2, :], vecs[:, 2, :], H_SCALE, None, ALU.mult))
            dve.wait_ge(tick, t)
            for n in range(NT - 2, NT):
                residual0(n, n % 2)
                make_shift(NG + n, 1)
                products1(n)
            dve.wait_ge(u_done, NT)
            nc.vector.tensor_scalar(u[:, :], u[:, :], bfbg[:, :], None, ALU.add).then_inc(u_done, 1)

            def value1(n, k):
                dve.wait_ge(v_ready, NT + n + 1)
                nc.vector.scalar_tensor_tensor(out=ps_v[k][:, :], in0=ps_v[k][:, :], scalar=1.0 / W_SCALE,
                                               in1=vecs[:, 2, :], op0=ALU.mult, op1=ALU.add).then_inc(v_biased, 1)
                value_lo(n, k, 1.0, NT)

            def weight_lo(i):
                dve.wait_ge(w_hi_done, 3 + i)
                split_lo(wl[i], ws[:, 0], ws[:, 1]).then_inc(w_split, 1)

            def query_lo(g):
                for c in range(C):
                    dve.wait_ge(q_ready, g * C + c + 1)
                    nc.vector.tensor_scalar(query_bank(g, c), query_bank(g, c), Q_SCALE / (H_SCALE * W_SCALE),
                                            q_bias[:, c:c + 1], ALU.mult, ALU.add).then_inc(q_biased, 1)
                    dve.wait_ge(q_hi_done, g * C + c + 1)
                    nc.vector.tensor_tensor(q_lo[:, c, :], query_bank(g, c), q_hi[:, c, :],
                                            ALU.subtract).then_inc(q_lo_done, 1)

            B = NT * NQ

            def masked1(n):
                at = B + n * NQ
                for q in range(NQ):
                    dve.wait_ge(s_relu, n * NJ + (q + 1) * BQ)
                    until(dve, mask_done, at + q + 1)
                    s = slice(q * QW, (q + 1) * QW)
                    nc.vector.tensor_tensor_reduce(out=score[:, s], in0=score[:, s], in1=mask_sb[:, q % 2, :],
                                                   scale=1.0, scalar=-3e38, op0=ALU.subtract, op1=ALU.max,
                                                   accum_out=qmax[:, q:q + 1]).then_inc(z_done, 1)
                dve.wait_ge(z_done, at + NQ)
                quarters_max().then_inc(max_chain, 1)
                dve.wait_ge(max_chain, 3 * NT + 2 * n + 1)
                nc.vector.tensor_scalar(neg_max[:, :], rowmax[:, 0:1], -1.0 / S_SCALE, None,
                                        ALU.mult).then_inc(max_chain, 1)

            def final(n, r):
                dve.wait_ge(pv_done, B + n * NQ + NQ)
                dve.wait_ge(xres_in[r], NT // 2 * 16 + (n - r) * 8 + 16)
                nc.vector.scalar_tensor_tensor(out=xres[:, r, :], in0=ps_o[r][:, :], scalar=rinv[:, r:r + 1],
                                               in1=xres[:, r, :], op0=ALU.mult, op1=ALU.add).then_inc(y_final, 1)

            def layer1(n, r4, queries):
                for q in range(NQ):
                    p_lo(q, B + n * NQ)
                row_sum(NT + n)
                inverse_sum(NT + n, r4 % 2)
                if not (isinstance(n, int) and n == 0):
                    final(n - 1, (r4 + 1) % 2)
                if not (isinstance(n, int) and n == NT - 1):
                    masked1(n + 1)
                if queries is not None:
                    query_lo(queries)

            in_threes(dve, 0, 6, value1)
            weight_lo(0)
            in_threes(dve, 6, 12, value1)
            weight_lo(1)
            in_threes(dve, 12, V1_M, value1)
            for c in range(C):
                dve.wait_ge(m_hi_done, c + 1)
                nc.vector.scalar_tensor_tensor(out=M_lo[:, c, :], in0=ps_s[c][:, :], scalar=1.0 / W_SCALE,
                                               in1=M_hi[:, c, :], op0=ALU.mult, op1=ALU.subtract).then_inc(m_lo_done, 1)
            in_threes(dve, V1_M, V1_Q, value1)
            query_lo(0)
            in_threes(dve, V1_Q, NT - 2, value1)
            value1(NT - 2, 0)
            value1(NT - 1, 1)
            masked1(0)
            for r in range(4):
                layer1(r, r, 1 if r == 2 else None)
            with dve.Fori(1, NT // 4 - 1, 1) as g:
                for r in range(4):
                    layer1(g * 4 + r, r, g + 1 if r == 2 else None)
            for r in range(4):
                layer1(NT - 4 + r, r, None)
            dve.wait_ge(sum_chain, 2 * 2 * NT)
            final(NT - 1, 1)

        @block.tensor
        def _(pe):
            def product(ps, a_hi, a_lo, b_hi, b_lo, start, stop):
                nc.tensor.matmul(ps, a_hi, b_hi, start=start, stop=False)
                nc.tensor.matmul(ps, a_hi, b_lo, start=False, stop=False)
                return nc.tensor.matmul(ps, a_lo, b_hi, start=False, stop=stop)

            def spread(i):
                pe.wait_ge(spread_in, i + 1)
                at_least(pe, spread_used, i)
                nc.tensor.matmul(ps_row[:, :], ones, diag, start=True, stop=True).then_inc(spread_out, 1)

            def values(n, k, at, W):
                at_least(pe, v_lo_done, at + n - 2)
                rows_n = bass.ds(n * P, P)
                for c in range(C):
                    done = product(ps_v[k][:, :], K_hi[:, c, rows_n], K_lo[:, c, rows_n], W[:, 0, c, :], W[:, 1, c, :],
                                   c == 0, c == C - 1)
                done.then_inc(v_ready, 1)

            def values0(n, k):
                values(n, k, 0, W0_16)

            def group0(g, g2):
                if not (isinstance(g, int) and g == 0):
                    for k in range(VG):
                        values0((g - 1) * VG + k, k)
                for r in range(4):
                    pe.wait_ge(h0_out[4 * g2 + r], (g - g2) * 8 + 16)
                at_least(pe, f_done, g)
                if isinstance(g, int) and g == 0:
                    pe.wait_ge(w12_done, 1)
                for r in range(4):
                    rows_n = bass.ds((g * 4 + r) * P, P)
                    for c in range(C):
                        done = product(ps_f[:, 2 * r:2 * r + 2], K_hi[:, c, rows_n], K_lo[:, c, rows_n],
                                       w12[:, 0, c, :], w12[:, 1, c, :], c == 0, c == C - 1)
                done.then_inc(f_ready, 1)
                if isinstance(g, int) and g == 0:
                    spread(0)
                    pe.wait_ge(w_split, 1)
                else:
                    spread(g)

            pe.wait_ge(consts, 4)
            grouped_tiles(pe, group0)
            in_threes(pe, V_TAIL, V_TAIL + 3, values0)
            spread(NG)
            in_threes(pe, V_TAIL + 3, NT - 2, values0)
            values0(NT - 2, 0)
            values0(NT - 1, 1)

            def weighted_values(n, r, at):
                for q in range(NQ):
                    pe.wait_ge(pt_in[q], at * 4 + 16)
                    if q == NQ - 1 and isinstance(at, int) and at == 0:
                        pe.wait_ge(v_lo_done, NT)
                    for j in range(q * JQ, (q + 1) * JQ):
                        last = product(ps_o[r][:, :], PT[:, q, 0, j % JQ, :], PT[:, q, 1, j % JQ, :],
                                       V_hi[:, j, :], V_lo[:, j, :], j == 0, j == NT - 1)
                    last.then_inc(pv_done, 1)

            pe.wait_ge(v_lo_done, NT - 1)

            def layer0(n, r):
                at_least(pe, o_relu, n - 1)
                weighted_values(n, r, n * NQ)

            paired_tiles(pe, layer0)

            pe.wait_ge(w_split, 2)
            pe.wait_ge(o_relu, NT - 1)

            def values1(n, k):
                pe.wait_ge(h_hi_done, NT + n + 2)
                values(n, k, NT, W1_16)

            values1(0, 0)
            pe.wait_ge(o_relu, NT)
            values1(1, 1)
            values1(2, 2)
            in_threes(pe, 3, V1_M, values1)
            for i in range(2):
                pe.wait_ge(wt_in[i], 8 * 16)
            for d in range(C):
                for c in range(C):
                    k = slice(d * P, (d + 1) * P)
                    last = product(ps_s[d][:, :], sh16[:, 0, 0, c, k], sh16[:, 0, 1, c, k],
                                   sh16[:, 1, 0, c, :], sh16[:, 1, 1, c, :], c == 0, c == C - 1)
                last.then_inc(m_ready, 1)
            in_threes(pe, V1_M, V1_Q, values1)

            def query(g):
                for d in range(C):
                    at_least(pe, q_lo_done, g * C + d - 1 if not isinstance(g, int) or g > 1 or d > 1 else 0)
                    for c in range(C):
                        k = slice(d * P, (d + 1) * P)
                        i = bass.ds(g * D, D)
                        last = product(query_bank(g, d), M_hi[:, c, k], M_lo[:, c, k], K_hi[:, c, i], K_lo[:, c, i],
                                       c == 0, c == C - 1)
                    last.then_inc(q_ready, 1)

            def scores(n, r4, g):
                pe.wait_ge(q_lo_done, g * C + C)
                for j in range(NJ):
                    at_least(pe, s_relu, n * NJ + j - 3)
                    i = slice(r4 * P, (r4 + 1) * P)
                    k = slice(j * JB, (j + 1) * JB)
                    for c in range(C):
                        last = product(ps_s[j % 4][:, :], q_hi[:, c, i], q_lo[:, c, i], K_hi[:, c, k], K_lo[:, c, k],
                                       c == 0, c == C - 1)
                    last.then_inc(s_ready, 1)

            pe.wait_ge(m_lo_done, C)
            query(0)
            in_threes(pe, V1_Q, NT - 2, values1)
            values1(NT - 2, 0)
            pe.wait_ge(h1_out, NT * 16)
            values(NT - 1, 1, NT, W1_16)
            scores(0, 0, 0)

            def layer1(n, r4, g, queries):
                if not (isinstance(n, int) and n == NT - 1):
                    scores(n + 1, (r4 + 1) % 4, g + 1 if r4 == 3 else g)
                if isinstance(n, int) and n == 0:
                    pe.wait_ge(v_lo_done, 2 * NT)
                if queries is not None:
                    query(queries)
                at_least(pe, y_final, n - 1)
                weighted_values(n, r4 % 2, NT * NQ + n * NQ)

            for r in range(4):
                layer1(r, r, 0, 1 if r == 2 else None)
            with pe.Fori(1, NT // 4 - 1, 1) as g:
                for r in range(4):
                    layer1(g * 4 + r, r, g, g + 1 if r == 2 else None)
            for r in range(4):
                layer1(NT - 4 + r, r, NT // 4 - 1, None)


_INS = ['x', 'adj', 'L0_gnn_W', 'L0_gnn_a1', 'L0_gnn_a2', 'L1_gnn_Wf', 'L1_gnn_bf', 'L1_gnn_Wg', 'L1_gnn_bg',
        'L1_gnn_W', 'L1_gnn_bW']


def kernel(**inputs):
    import numpy as _np
    import concourse.bacc as _bacc
    from concourse import mybir as _mybir
    from concourse.bass_utils import run_bass_kernel_spmd as _run

    nc = _bacc.Bacc("TRN2", target_bir_lowering=False, num_devices=1)
    arrays, args = {}, []
    for name in _INS:
        a = _np.ascontiguousarray(inputs[name])
        arrays[f"in_{name}_dram"] = a
        args.append(nc.dram_tensor(f"in_{name}_dram", a.shape, _mybir.dt.from_np(a.dtype), kind="ExternalInput").ap())
    out = nc.dram_tensor("out_dram", inputs['x'].shape, _mybir.dt.float32, kind="ExternalOutput").ap()
    graph_layers(nc, *args, out)
    r = _run(nc, [arrays], core_ids=[0])
    return r.results[0]["out_dram"]
```

```python
from contextlib import ExitStack

import concourse.bass as bass
from concourse import mybir

F32 = mybir.dt.float32
F16 = mybir.dt.float16
BF16 = mybir.dt.bfloat16
I32 = mybir.dt.int32
ALU = mybir.AluOpType
ACT = mybir.ActivationFunctionType
AX_X = mybir.AxisListType.X

P = 128
SLOPE = 0.2
EPS = 1e-5

H_SCALE = 2.0 ** 10
W_SCALE = 2.0 ** 12
Q_SCALE = 2.0 ** 9
S_SCALE = Q_SCALE * H_SCALE
P_SCALE = 2.0 ** 14
MASK = 9e15 * S_SCALE


def graph_layers(nc, x, adj, W0, a1, a2, Wf, bf, Wg, bg, W1, bW, out):
    N, D = x.shape
    NT = N // P
    C = D // P
    NQ = 4
    QW = N // NQ
    JQ = QW // P
    JB = 512
    NJ = N // JB
    BQ = QW // JB

    x1 = nc.dram_tensor("x1_scratch", [N, D], F32, kind="Internal").ap()

    with ExitStack() as ctx:
        def sb(name, shape, dt):
            return ctx.enter_context(nc.sbuf_tensor(name, shape, dt))

        def sem(name):
            return ctx.enter_context(nc.semaphore(name))

        V_hi = sb("V_hi", [P, NT, D], F16)
        V_lo = sb("V_lo", [P, NT, D], F16)
        K = sb("K", [P, 2, C, N], F16)
        adj_sb = sb("adj_sb", [P, 2, QW], I32)
        mask_sb = sb("mask_sb", [P, 2, QW], BF16)
        score = sb("score", [P, N], F32)
        p_nat = sb("p_nat", [P, 2, 2, QW], F16)
        PT = sb("PT", [P, NQ, 2, JQ, P], F16)
        shared = sb("shared", [P, N], F32)
        xres = sb("xres", [P, 2, D], F32)
        work = sb("work", [P, D], F32)
        h_nat = sb("h_nat", [P, 2, D], F16)
        u_row = sb("u_row", [P, D], F32)
        f1 = sb("f1", [P, NT], F32)
        u = sb("u", [P, NT], F32)
        dots = sb("dots", [P, 1], F32)
        q_bias = sb("q_bias", [P, C], F32)
        vec_col = sb("vec_col", [P, 3, C], F32)
        w12 = sb("w12", [P, C, 4], F16)
        pick = sb("pick", [P, 2], F32)
        bfbg = sb("bfbg", [P, 1], F32)
        stats = sb("stats", [P, 4, 6], F32)
        mean_var = sb("mean_var", [P, 4, 2], F32)
        ve = sb("ve", [P, 4], F32)
        rstd = sb("rstd", [P, 4], F32)
        shift = sb("shift", [P, 4], F32)
        mhalf = sb("mhalf", [P, 4], F32)
        ones4 = sb("ones4", [P, NQ], F32)
        mask_bias = sb("mask_bias", [P, 1], F32)
        qmax = sb("qmax", [P, NQ], F32)
        rowmax = sb("rowmax", [P, 2], F32)
        neg_max = sb("neg_max", [P, 1], F32)
        qsum = sb("qsum", [P, NQ], F32)
        qweighed = sb("qweighed", [P, NQ], F32)
        rowsum = sb("rowsum", [P, 1], F32)
        rinv = sb("rinv", [P, 2], F32)

        def f32_rows(region):
            return region.bitcast(F32).rearrange("p (c n) -> p c n", n=D)

        K_hi, K_lo = K[:, 0], K[:, 1]
        K_blocks = K[:, :, :, :].rearrange("p s c n -> p (s c) n")
        pt_flat = PT[:, :, :, :, :].rearrange("p q s j i -> p (q s j i)")
        w_f32 = score[:, 0:C * D].rearrange("p (c n) -> p c n", c=C)
        W0_16 = pt_flat[:, 2 * C * D:4 * C * D].rearrange("p (s c n) -> p s c n", s=2, c=C)
        w1_f32 = shared[:, 0:C * D].rearrange("p (c n) -> p c n", c=C)
        W1_16 = score[:, C * D:2 * C * D].bitcast(F16).rearrange("p (s c n) -> p s c n", s=2, c=C)
        vecs = f32_rows(adj_sb[:, :, :].rearrange("p a b -> p (a b)"))
        v_tail = [V[:, NT // 2:NT, :].rearrange("p a b -> p (a b)") for V in (V_hi, V_lo)]
        wf_nat = f32_rows(v_tail[0][:, 0:2 * C * D])
        wg_nat = f32_rows(v_tail[0][:, 2 * C * D:4 * C * D])
        xin = [f32_rows(pt_flat[:, 0:2 * C * D]), f32_rows(v_tail[1][:, 2 * C * D:4 * C * D])]
        pn32 = p_nat[:, :, :, :].rearrange("p a b c -> p (a b c)").bitcast(F32)
        diag = pn32[:, 0:D]
        junk = pn32[:, D:2 * D]
        ident = pn32[:, 2 * D:2 * D + P]
        ones = pn32[:, 2 * D + P:2 * D + 2 * P]
        pick_f2 = pn32[0:4, 2 * D + 2 * P:2 * D + 3 * P]
        f_rows = pn32[0:4, 3 * D:4 * D]
        h_f32 = [score[:, C * D + r * D:C * D + (r + 1) * D] for r in range(4)]
        h_halves = [h_nat[:, :, :]] + [t.bitcast(F16).rearrange("p (s n) -> p s n", s=2)
                                       for t in (work[:, :], xres[:, 0, :], xres[:, 1, :])]
        wl = [f32_rows(pt_flat[:, i * 2 * C * D:(i + 1) * 2 * C * D]) for i in range(2)]
        ws = p_nat[:, :, :, :].rearrange("p a b (c n) -> p a (b c) n", n=D)
        sh16 = shared[:, :].bitcast(F16).rearrange("p (m s c n) -> p m s c n", m=2, s=2, c=C)
        M_hi, M_lo = sh16[:, 0, 0], sh16[:, 0, 1]
        q_hi, q_lo = sh16[:, 1, 0], sh16[:, 1, 1]

        ps_o = [ctx.enter_context(nc.psum_tensor(f"ps_o{i}", [P, D], F32)) for i in range(2)]
        ps_q = [ctx.enter_context(nc.psum_tensor(f"ps_q{i}", [P, D], F32)) for i in range(2)]
        ps_s = [ctx.enter_context(nc.psum_tensor(f"ps_s{i}", [P, JB], F32)) for i in range(4)]
        ps_v = [[ps_q[0], ps_q[1], ps_s[3]], [ps_q[0], ps_q[1], ps_o[0]]]

        V1_M, V1_Q, V1_S = 18, 24, 28
        ps_f, ps_row, ps_col = ps_s[0], ps_s[1], ps_s[2]

        NG = NT // 4
        V_TAIL = 3 * (NG - 1) + 1

        def group_values(g):
            if isinstance(g, int) and g < 2:
                return [(n, n % 3) for n in ((0, 1, 2), (3,))[g]]
            return [(g * 3 + (k - 2), (k + 1) % 3) for k in range(3)]

        def evacuated(g):
            if isinstance(g, int) and g < 3:
                return ([], group_values(0), group_values(1) + group_values(2)[:2])[g]
            return [(g * 3 - 3, 0)] + group_values(g)[:2]

        w0_in = sem("w0_in")
        params_in = sem("params_in")
        x_in = [sem(f"x_in{i}") for i in range(8)]
        xres_in = [sem(f"xres_in{i}") for i in range(2)]
        adj_in = [sem(f"adj_in{i}") for i in range(2)]
        h0_out = [sem(f"h0_out{i}") for i in range(8)]
        h1_out = sem("h1_out")
        pt_in = [sem(f"pt_in{q}") for q in range(NQ)]
        x1_out = [sem(f"x1_out{i}") for i in range(2)]
        y_out = [sem(f"y_out{i}") for i in range(2)]
        bw_done = sem("bw_done")
        w1_in = sem("w1_in")
        w1_moved = sem("w1_moved")
        wfg_in = sem("wfg_in")
        wt_in = [sem(f"wt_in{i}") for i in range(2)]
        stood = sem("stood")
        consts = sem("consts")
        zeroed = sem("zeroed")
        tick = sem("tick")
        w_hi_done = sem("w_hi_done")
        w_split = sem("w_split")
        picks_done = sem("picks_done")
        spread_out = sem("spread_out")
        spread_used = sem("spread_used")
        u_diag = sem("u_diag")
        u_spread = sem("u_spread")
        u_row_done = sem("u_row_done")
        bn_done = sem("bn_done")
        aggr_done = sem("aggr_done")
        ve_done = sem("ve_done")
        rstd_done = sem("rstd_done")
        shift_done = sem("shift_done")
        h_done = sem("h_done")
        h_hi_done = sem("h_hi_done")
        h_lo_done = sem("h_lo_done")
        h_used = sem("h_used")
        u_done = sem("u_done")
        vectors_done = sem("vectors_done")
        w12_hi = sem("w12_hi")
        w12_done = sem("w12_done")
        f_ready = sem("f_ready")
        f_done = sem("f_done")
        v_ready = sem("v_ready")
        v_biased = sem("v_biased")
        v_hi_done = sem("v_hi_done")
        v_lo_done = sem("v_lo_done")
        mask_done = sem("mask_done")
        z_done = sem("z_done")
        max_chain = sem("max_chain")
        y0_done = sem("y0_done")
        y_done = sem("y_done")
        leaky_done = sem("leaky_done")
        exp_done = sem("exp_done")
        p_hi_done = sem("p_hi_done")
        p_lo_done = sem("p_lo_done")
        sum_chain = sem("sum_chain")
        pv_done = sem("pv_done")
        o_relu = sem("o_relu")
        x1_done = sem("x1_done")
        y_final = sem("y_final")
        m_ready = sem("m_ready")
        m_hi_done = sem("m_hi_done")
        m_lo_done = sem("m_lo_done")
        q_ready = sem("q_ready")
        q_biased = sem("q_biased")
        q_hi_done = sem("q_hi_done")
        q_lo_done = sem("q_lo_done")
        s_ready = sem("s_ready")
        s_relu = sem("s_relu")

        def at_least(eng, semaphore, value):
            if not isinstance(value, int) or value > 0:
                eng.wait_ge(semaphore, value)

        def query_bank(g, c):
            return (ps_s[c] if isinstance(g, int) and g == 0 else ps_q[c % 2])[:, :]

        def until(eng, semaphore, value):
            if isinstance(value, int):
                at_least(eng, semaphore, value)
            else:
                eng.wait_ge(semaphore, value).then_inc(stood, 1)

        def in_threes(eng, lo, hi, body):
            with eng.Fori(lo // 3, hi // 3, 1) as three:
                for k in range(3):
                    body(three * 3 + k, k)

        def in_pairs(eng, count, body, peeled=1):
            for n in range(2 * peeled):
                body(n, n % 2)
            with eng.Fori(peeled, count // 2 - 1, 1) as pair:
                for r in range(2):
                    body(pair * 2 + r, r)
            body(count - 2, 0)
            body(count - 1, 1)

        def rows(t, n):
            return t[bass.ds(n * P, P), :]

        block = ctx.enter_context(nc.Block())

        @block.sync
        def _(sp):
            def broadcast(v):
                return v.rearrange("(a n) -> a n", a=1).broadcast_to([P, D])

            def load_x(n, r4, g2):
                sp.dma_start(xin[g2][:, r4, :], rows(x, n)).then_inc(x_in[4 * g2 + r4], 16)

            for n in range(4):
                load_x(n, n, 0)
            sp.dma_start(w_f32, W0.rearrange("(c p) n -> p c n", p=P)).then_inc(w0_in, 16)
            for i, v in enumerate((a1, a2)):
                sp.dma_start(vecs[:, i, :], broadcast(v.rearrange("a b -> (a b)"))).then_inc(w0_in, 16)
            for n in range(4):
                load_x(n + 4, n, 1)

            def group0(g, g2):
                for r in range(4):
                    n = g * 4 + r
                    until(sp, h_hi_done, n + 1)
                    until(sp, h_lo_done, n + 1)
                    if r == 0:
                        until(sp, f_ready, g - 1)
                    sp.dma_start_transpose(K_blocks[:, :, bass.ds(n * P, P)],
                                           h_halves[r].rearrange("p s n -> p (s n)")).then_inc(h0_out[4 * g2 + r], 16)
                if not (isinstance(g, int) and g >= NG - 2):
                    for r in range(4):
                        load_x(g * 4 + (r + 8), r, g2)
                if isinstance(g, int) and g == 0:
                    for i, v in enumerate((bf, bg)):
                        sp.dma_start(vecs[:, 2 + i, :], broadcast(v)).then_inc(params_in, 16)
                    sp.dma_start(wf_nat, Wf.rearrange("(c p) n -> p c n", p=P)).then_inc(params_in, 16)
                    sp.dma_start(wg_nat, Wg.rearrange("(c p) n -> p c n", p=P)).then_inc(params_in, 16)

            in_pairs(sp, NG, group0)

            sp.wait_ge(vectors_done, 1)

            def load_adj(n, q, at):
                until(sp, mask_done, at + q - 1)
                sp.dma_start(adj_sb[:, q % 2, :], adj[bass.ds(n * P, P), q * QW:(q + 1) * QW]).then_inc(adj_in[q % 2], 16)

            def transpose_p(q, at):
                until(sp, p_lo_done, at + q + 1)
                until(sp, pv_done, at - NQ + q + 1)
                sp.dma_start_transpose(PT[:, q].rearrange("p s j i -> p (s j) i"),
                                       p_nat[:, q % 2].rearrange("p s n -> p (s n)")).then_inc(pt_in[q], 16)

            def store_x1(n, r):
                until(sp, x1_done, n + 1)
                sp.dma_start(rows(x1, n), xres[:, r, :]).then_inc(x1_out[r], 16)

            def load_xres(n, r, stored):
                if stored is not None:
                    sp.wait_ge(x1_out[r], stored)
                    until(sp, h_done, NT + n - 1)
                sp.dma_start(xres[:, r, :], rows(x, n)).then_inc(xres_in[r], 16)

            def transpose_h1(n):
                until(sp, h_hi_done, NT + n + 1)
                until(sp, h_lo_done, NT + n + 1)
                sp.dma_start_transpose(K_blocks[:, :, bass.ds(n * P, P)],
                                       h_nat[:, :, :].rearrange("p s n -> p (s n)")).then_inc(h1_out, 16)

            load_adj(0, 0, 0)
            load_adj(0, 1, 0)
            load_adj(0, 2, 0)
            load_adj(0, 3, 0)
            load_adj(1, 0, NQ)
            load_adj(1, 1, NQ)
            for r in range(4):
                sp.wait_ge(h0_out[4 + r], NG // 2 * 16)
            load_xres(0, 0, None)
            load_xres(1, 1, None)

            def layer0(n, r):
                early = isinstance(n, int) and n < 2
                last = isinstance(n, int) and n == NT - 1
                if last:
                    sp.wait_ge(z_done, NT * NQ)
                    sp.dma_start(w1_f32, W1.rearrange("(c p) n -> p c n", p=P)).then_inc(w1_in, 16)
                transpose_p(0, n * NQ)
                if not last:
                    load_adj(n + 1, 2, n * NQ + NQ)
                transpose_p(1, n * NQ)
                if not last:
                    load_adj(n + 1, 3, n * NQ + NQ)
                if not early:
                    store_x1(n - 2, r)
                    transpose_h1(n - 2)
                if isinstance(n, int) and n == 0:
                    sp.wait_ge(v_ready, NT)
                if last:
                    sp.dma_start(vecs[:, 2, :], bW.rearrange("(a n) -> a n", a=1).broadcast_to([P, D])).then_inc(w1_in, 16)
                    sp.dma_start(adj_sb[:, 0, :], adj[0:P, 0:QW]).then_inc(adj_in[0], 16)
                transpose_p(2, n * NQ)
                if not (isinstance(n, int) and n >= NT - 2):
                    load_adj(n + 2, 0, n * NQ + 2 * NQ)
                transpose_p(3, n * NQ)
                if not (isinstance(n, int) and n >= NT - 2):
                    load_adj(n + 2, 1, n * NQ + 2 * NQ)
                if not early:
                    load_xres(n, r, (n - r) * 8)

            in_pairs(sp, NT, layer0)

            for n in range(NT - 2, NT):
                store_x1(n, n % 2)
                transpose_h1(n)
            sp.wait_ge(pv_done, NT * NQ)
            for i, w in enumerate((Wf, Wg)):
                sp.dma_start(wl[i], w.rearrange("(c p) n -> p c n", p=P)).then_inc(wfg_in, 16)
            for i in range(2):
                sp.wait_ge(w_split, 2 + i + 1)
                for half in range(2):
                    for c in range(C):
                        sp.dma_start_transpose(sh16[:, i, half, :, c * P:(c + 1) * P],
                                               ws[:, half, c, :]).then_inc(wt_in[i], 16)

            sp.dma_start(W0_16, W1_16).then_inc(w1_moved, 16)

            B = NT * NQ
            sp.wait_ge(bw_done, 1)
            sp.dma_start(adj_sb[:, 1, :], adj[0:P, QW:2 * QW]).then_inc(adj_in[1], 16)
            load_adj(0, 2, B)
            load_adj(0, 3, B)
            load_adj(1, 0, B + NQ)
            load_adj(1, 1, B + NQ)
            for r in range(2):
                sp.wait_ge(x1_out[r], NT // 2 * 16)
                sp.wait_ge(h_done, 2 * NT)
                sp.dma_start(xres[:, r, :], x1[r * P:(r + 1) * P, :]).then_inc(xres_in[r], 16)

            def layer1(n, r):
                for q in range(NQ):
                    if isinstance(n, int) and n == 0 and q == 2:
                        sp.wait_ge(v_ready, 2 * NT)
                    transpose_p(q, B + n * NQ)
                if not (isinstance(n, int) and n == NT - 1):
                    load_adj(n + 1, 2, B + n * NQ + NQ)
                    load_adj(n + 1, 3, B + n * NQ + NQ)
                if not (isinstance(n, int) and n == 0):
                    m, s = n - 1, 1 - r
                    until(sp, y_final, n)
                    sp.dma_start(rows(out, m), xres[:, s, :]).then_inc(y_out[s], 16)
                if not (isinstance(n, int) and n >= NT - 2):
                    load_adj(n + 2, 0, B + n * NQ + 2 * NQ)
                    load_adj(n + 2, 1, B + n * NQ + 2 * NQ)
                if not (isinstance(n, int) and (n == 0 or n == NT - 1)):
                    m, s = n - 1, 1 - r
                    sp.wait_ge(y_out[s], (m - s) * 8 + 16)
                    sp.dma_start(xres[:, s, :], rows(x1, n + 1)).then_inc(xres_in[s], 16)

            in_pairs(sp, NT, layer1)
            sp.wait_ge(y_final, NT)
            sp.dma_start(rows(out, NT - 1), xres[:, 1, :]).then_inc(y_out[1], 16)
            for r in range(2):
                sp.wait_ge(y_out[r], NT // 2 * 16)

        @block.gpsimd
        def _(pool):
            nc.gpsimd.memset(ident, 0.0).then_inc(zeroed, 1)
            nc.gpsimd.memset(ones, 1.0).then_inc(consts, 1)
            nc.gpsimd.memset(mhalf[:, :], -0.5).then_inc(zeroed, 1)
            nc.gpsimd.memset(ones4[:, :], 1.0).then_inc(consts, 1)
            nc.gpsimd.memset(mask_bias[:, :], MASK).then_inc(consts, 1)
            pool.wait_ge(zeroed, 2)
            nc.gpsimd.affine_select(out=ident, in_=ident, compare_op=ALU.not_equal, fill=1.0, base=0,
                                    pattern=[[-1, P]], channel_multiplier=1).then_inc(consts, 1)
            def inverse_deviation(k, tiles, used):
                s = slice(0, tiles)
                until(pool, aggr_done, k + 1)
                nc.gpsimd.tensor_scalar(ve[:, s], mean_var[:, s, 1], EPS, H_SCALE ** -2,
                                        ALU.add, ALU.mult).then_inc(ve_done, 1)
                pool.wait_ge(ve_done, k + 1)
                at_least(pool, h_done, used)
                nc.gpsimd.tensor_tensor(rstd[:, s], ve[:, s], mhalf[:, s], ALU.pow).then_inc(rstd_done, 1)

            inverse_deviation(0, 4, 0)
            with pool.Fori(1, NG, 1) as g:
                inverse_deviation(g, 4, g * 4)
            with pool.Fori(0, NT, 1) as n:
                inverse_deviation(n + NG, 1, n + NT)

        @block.scalar
        def _(act):
            def split_hi(w, hi, loaded, value, done):
                act.wait_ge(loaded, value)
                nc.scalar.mul(hi, w, W_SCALE).then_inc(done, 1)

            def value_hi(n, k):
                act.wait_ge(v_ready, n + 1)
                nc.scalar.activation(V_hi[:, bass.ds(n, 1), :], ps_v[0][k][:, :].rearrange("p (a n) -> p a n", a=1),
                                     ACT.Copy, scale=1.0 / W_SCALE).then_inc(v_hi_done, 1)

            def spread_end(g):
                act.wait_ge(spread_out, g + 1)
                nc.scalar.copy(shared[:, bass.ds(g * D, D)], ps_row[:, :])
                nc.scalar.copy(f1[:, bass.ds(g * 4, 4)], ps_col[:, 0:4]).then_inc(spread_used, 1)

            def take_f(g):
                if not (isinstance(g, int) and g == 0):
                    spread_end(g - 1)
                act.wait_ge(f_ready, g + 1)
                nc.scalar.activation(f_rows, ps_f[0:4, :], ACT.Copy,
                                     scale=1.0 / (H_SCALE * W_SCALE)).then_inc(f_done, 1)

            def group0(g, g2):
                first = isinstance(g, int) and g == 0

                def relu_h(r):
                    n = g * 4 + r
                    if r == 0:
                        act.wait_ge(shift_done, g + 1)
                    at_least(act, h_lo_done, n - 3)
                    nc.scalar.activation(h_f32[r], xin[g2][:, r, :], ACT.Relu, bias=shift[:, r:r + 1],
                                         scale=rstd[:, r:r + 1]).then_inc(h_done, 1)

                def high_half(r):
                    act.wait_ge(h_done, g * 4 + (r + 1))
                    if not first:
                        act.wait_ge(h0_out[4 * (1 - g2) + r], (g - g2) * 8 + 16 * g2)
                    nc.scalar.copy(h_halves[r][:, 0, :], h_f32[r]).then_inc(h_hi_done, 1)

                for r in (0, 2):
                    relu_h(r)
                    relu_h(r + 1)
                    high_half(r)
                    high_half(r + 1)
                    if first and r == 0:
                        split_hi(w_f32, W0_16[:, 0], w0_in, 3 * 16, w_hi_done)
                if not first:
                    take_f(g - 1)
                for v in evacuated(g):
                    value_hi(*v)

            in_pairs(act, NG, group0, peeled=2)

            def mask(q, at):
                act.wait_ge(adj_in[q % 2], at * 8 + 16 * (q // 2 + 1))
                at_least(act, z_done, at + q - 1)
                nc.scalar.activation(mask_sb[:, q % 2, :], adj_sb[:, q % 2, :], ACT.Relu,
                                     bias=mask_bias[:, :], scale=-MASK).then_inc(mask_done, 1)

            def exp_quarter(q, at, scale):
                nc.scalar.activation(score[:, q * QW:(q + 1) * QW], score[:, q * QW:(q + 1) * QW], ACT.Exp,
                                     bias=neg_max[:, :], scale=scale,
                                     accum_out=qsum[:, q:q + 1]).then_inc(exp_done, 1)

            def p_hi(q, at):
                act.wait_ge(exp_done, at + q + 1)
                if q >= 2:
                    act.wait_ge(pt_in[q - 2], at * 4 + 16)
                else:
                    at_least(act, pt_in[q + 2], at * 4)
                nc.scalar.mul(p_nat[:, q % 2, 0, :], score[:, q * QW:(q + 1) * QW], P_SCALE).then_inc(p_hi_done, 1)

            def add_f1(n, q):
                s = slice(q * QW, (q + 1) * QW)
                until(act, z_done, n * NQ + q + 1)
                nc.scalar.activation(score[:, s], score[:, s], ACT.Identity,
                                     bias=f1[:, bass.ds(n, 1)]).then_inc(y_done, 1)

            def relu_out(n, r):
                act.wait_ge(pv_done, n * NQ + NQ)
                act.wait_ge(sum_chain, 2 * n + 2)
                at_least(act, h_used, n)
                nc.scalar.activation(work[:, :], ps_o[r][:, :], ACT.Relu, scale=rinv[:, r:r + 1]).then_inc(o_relu, 1)

            def norm1(n, r):
                act.wait_ge(shift_done, NG + n + 1)
                nc.scalar.activation(work[:, :], xres[:, r, :], ACT.Relu, bias=shift[:, 0:1],
                                     scale=rstd[:, 0:1]).then_inc(h_done, 1)
                act.wait_ge(h_done, NT + n + 1)
                at_least(act, h1_out, n * 16)
                nc.scalar.copy(h_nat[:, 0, :], work[:, :]).then_inc(h_hi_done, 1)

            tail = iter(range(V_TAIL + 3, NT))

            def spare(count=1):
                for _, v in zip(range(count), tail):
                    value_hi(v, v % 3)

            def layer0(n, r):
                first = isinstance(n, int) and n == 0
                early = isinstance(n, int) and n < 2
                last = isinstance(n, int) and n == NT - 1
                at = n * NQ
                if not early:
                    relu_out(n - 2, r)
                if first:
                    act.wait_ge(u_row_done, 1)
                at_least(act, sum_chain, 2 * n - 1)
                act.wait_ge(max_chain, 3 * n + 3)
                for q in range(2):
                    act.wait_ge(leaky_done, at + q + 1)
                    exp_quarter(q, at, 1.0)
                p_hi(0, at)
                if not last:
                    mask(0, at + NQ)
                if first:
                    spare()
                act.wait_ge(leaky_done, at + 3)
                exp_quarter(2, at, 1.0)
                p_hi(1, at)
                if not last:
                    mask(1, at + NQ)
                if first:
                    spare()
                act.wait_ge(leaky_done, at + 4)
                exp_quarter(3, at, 1.0)
                p_hi(2, at)
                if first:
                    spare()
                if not early:
                    norm1(n - 2, r)
                if not last:
                    mask(2, at + NQ)
                p_hi(3, at)
                if first:
                    spare()
                if not last:
                    add_f1(n + 1, 1)
                    mask(3, at + NQ)
                    add_f1(n + 1, 2)
                    add_f1(n + 1, 3)
                if first:
                    spare(NT)

            value_hi(*group_values(NG - 1)[2])
            mask(0, 0)
            mask(1, 0)
            take_f(NG - 1)
            last_values = [(n, n % 3) for n in range(V_TAIL, V_TAIL + 3)]
            value_hi(*last_values[0])
            spread_end(NG - 1)
            value_hi(*last_values[1])
            mask(2, 0)
            add_f1(0, 1)
            value_hi(*last_values[2])
            mask(3, 0)
            add_f1(0, 2)
            add_f1(0, 3)
            spare(3)
            in_pairs(act, NT, layer0)

            act.wait_ge(p_lo_done, NT * NQ)
            split_hi(w1_f32, W1_16[:, 0], w1_in, 2 * 16, w_hi_done)
            for n in range(NT - 2, NT):
                relu_out(n, n % 2)
                norm1(n, n % 2)

            def value_hi1(n, k):
                act.wait_ge(v_biased, n + 1)
                nc.scalar.copy(V_hi[:, bass.ds(n, 1), :],
                               ps_v[1][k][:, :].rearrange("p (a n) -> p a n", a=1)).then_inc(v_hi_done, 1)

            def weight_hi(i):
                act.wait_ge(wfg_in, 2 * 16)
                if i:
                    act.wait_ge(wt_in[0], 8 * 16)
                nc.scalar.mul(ws[:, 0], wl[i], W_SCALE).then_inc(w_hi_done, 1)

            def query_hi(g):
                for c in range(C):
                    act.wait_ge(q_biased, g * C + c + 1)
                    nc.scalar.copy(q_hi[:, c, :], query_bank(g, c)).then_inc(q_hi_done, 1)

            B = NT * NQ

            def relu_scores(n):
                at = B + n * NQ
                first = isinstance(n, int) and n == 0
                for q in range(NQ):
                    if not first:
                        mask(q, at)
                    act.wait_ge(p_lo_done, at - NQ + q + 1)
                    for b in range(BQ):
                        j = q * BQ + b
                        until(act, s_ready, n * NJ + j + 1)
                        nc.scalar.activation(score[:, j * JB:(j + 1) * JB], ps_s[j % 4][:, :], ACT.Relu,
                                             bias=u[:, bass.ds(n, 1)]).then_inc(s_relu, 1)
                    if first:
                        mask(q, at)

            def late_value(n, i):
                if isinstance(n, int) and n == 0:
                    value_hi1(V1_S + i, (V1_S + i) % 3)

            def layer1(n, r4, queries):
                at = B + n * NQ
                act.wait_ge(sum_chain, 2 * NT + 2 * n)
                act.wait_ge(max_chain, 3 * NT + 2 * n + 2)
                for q in range(2):
                    exp_quarter(q, at, 1.0 / S_SCALE)
                p_hi(0, at)
                for q in range(2, NQ):
                    late_value(n, q - 2)
                    exp_quarter(q, at, 1.0 / S_SCALE)
                    p_hi(q - 1, at)
                late_value(n, 2)
                p_hi(3, at)
                late_value(n, 3)
                if not (isinstance(n, int) and n == NT - 1):
                    relu_scores(n + 1)
                if queries is not None:
                    query_hi(queries)

            in_threes(act, 0, 6, value_hi1)
            weight_hi(0)
            in_threes(act, 6, 12, value_hi1)
            weight_hi(1)
            in_threes(act, 12, V1_M, value_hi1)
            act.wait_ge(m_ready, C)
            for c in range(C):
                nc.scalar.activation(M_hi[:, c, :], ps_s[c][:, :], ACT.Copy, scale=1.0 / W_SCALE).then_inc(m_hi_done, 1)
            in_threes(act, V1_M, V1_Q, value_hi1)
            query_hi(0)
            in_threes(act, V1_Q, V1_S - 1, value_hi1)
            value_hi1(V1_S - 1, (V1_S - 1) % 3)
            act.wait_ge(u_done, NT + 1)
            relu_scores(0)
            for r in range(4):
                layer1(r, r, 1 if r == 2 else None)
            with act.Fori(1, NT // 4 - 1, 1) as g:
                for r in range(4):
                    layer1(g * 4 + r, r, g + 1 if r == 2 else None)
            for r in range(4):
                layer1(NT - 4 + r, r, None)

        @block.vector
        def _(dve):
            ticks = [0]

            def ticked(ins):
                ins.then_inc(tick, 1)
                ticks[0] += 1
                return ticks[0]

            def split_lo(w, hi, lo):
                return nc.vector.scalar_tensor_tensor(out=lo, in0=w, scalar=W_SCALE, in1=hi,
                                                      op0=ALU.mult, op1=ALU.subtract)

            def dot(o, a, b, scale, acc):
                return nc.vector.tensor_tensor_reduce(out=o, in0=a, in1=b, scale=scale, scalar=0.0,
                                                      op0=ALU.mult, op1=ALU.add, accum_out=acc)

            def rank_one(pairs):
                t = ticks[0]
                for w, vec, scale, acc in pairs:
                    at_least(dve, tick, t)
                    t = ticked(dot(junk, w, vecs[:, vec, :], scale, acc))
                dve.wait_ge(tick, t)

            def aggregate(k, tiles, bn_count):
                dve.wait_ge(bn_done, bn_count)
                until(dve, rstd_done, k)
                until(dve, shift_done, k)
                for r in range(tiles):
                    last = nc.vector.bn_aggr(mean_var[:, r, :], stats[:, r, :])
                last.then_inc(aggr_done, 1)

            def statistics0(g, g2):
                for r in range(4):
                    dve.wait_ge(x_in[4 * g2 + r], (g - g2) * 8 + 16)
                    nc.vector.bn_stats(stats[:, r, :], xin[g2][:, r, :]).then_inc(bn_done, 1)
                aggregate(g, 4, g * 4 + 4)

            def make_shift(k, tiles):
                s = slice(0, tiles)
                dve.wait_ge(rstd_done, k + 1)
                nc.vector.scalar_tensor_tensor(out=shift[:, s], in0=mean_var[:, s, 0], scalar=-1.0,
                                               in1=rstd[:, s], op0=ALU.mult, op1=ALU.mult).then_inc(shift_done, 1)

            def value_lo(n, k, scale=1.0 / W_SCALE, layer=0):
                dve.wait_ge(v_hi_done, layer * NT + n + 1)
                nc.vector.scalar_tensor_tensor(out=V_lo[:, bass.ds(n, 1), :],
                                               in0=ps_v[layer][k][:, :].rearrange("p (a n) -> p a n", a=1), scalar=scale,
                                               in1=V_hi[:, bass.ds(n, 1), :],
                                               op0=ALU.mult, op1=ALU.subtract).then_inc(v_lo_done, 1)

            def group0(g, g2):
                first = isinstance(g, int) and g == 0
                last = isinstance(g, int) and g == NG - 1
                for r in range(4):
                    if first and r == 2:
                        dve.wait_ge(w0_in, 3 * 16)
                        dve.wait_ge(w_hi_done, 1)
                        split_lo(w_f32, W0_16[:, 0], W0_16[:, 1]).then_inc(w_split, 1)
                    dve.wait_ge(h_hi_done, g * 4 + (r + 1))
                    nc.vector.tensor_tensor(h_halves[r][:, 1, :], h_f32[r], h_halves[r][:, 0, :],
                                            ALU.subtract).then_inc(h_lo_done, 1)
                early = evacuated(g) if isinstance(g, int) and g < 3 else evacuated(g)[:1]
                for v in early:
                    value_lo(*v)
                if not last:
                    statistics0(g + 1, 1 - g2)
                if first:
                    weight_vector0(0)
                if not last:
                    make_shift(g + 1, 4)
                if first:
                    weight_vector0(1)
                    halve_vectors0()
                for v in evacuated(g)[len(early):]:
                    value_lo(*v)
                if not (first or last) and isinstance(g, int) and g <= 3:
                    vectors1(g)

            def weight_vector0(v):
                rank_one([(w_f32[:, c, :], v, W_SCALE, vec_col[:, v, c:c + 1]) for c in range(C)])

            def halve_vectors0():
                w12_f32 = vec_col[:, 0:2, :].rearrange("p v c -> p c v")
                nc.vector.tensor_copy(w12[:, :, 0:2], w12_f32).then_inc(w12_hi, 1)
                dve.wait_ge(w12_hi, 1)
                nc.vector.tensor_tensor(w12[:, :, 2:4], w12_f32, w12[:, :, 0:2], ALU.subtract).then_inc(w12_done, 1)
                nc.vector.tensor_tensor(pick[:, :], ident[:, 0:2], ident[:, 2:4], ALU.add).then_inc(picks_done, 1)
                dve.wait_ge(picks_done, 1)
                nc.vector.tensor_scalar(pick_f2, ones[0:4, :], pick[0:4, 1:2], None, ALU.mult).then_inc(picks_done, 1)

            def vectors1(part):
                dve.wait_ge(params_in, 4 * 16)
                if part == 1:
                    rank_one([(wf_nat[:, c, :], 3, 1.0, vec_col[:, 2, c:c + 1]) for c in range(C)])
                elif part == 2:
                    rank_one([(wg_nat[:, c, :], 2, Q_SCALE, q_bias[:, c:c + 1]) for c in range(C)])
                else:
                    rank_one([(vecs[:, 2, :], 3, S_SCALE, bfbg[:, :])])
                    for c in range(C):
                        last = nc.vector.tensor_scalar(diag[:, c * P:(c + 1) * P], ident, vec_col[:, 2, c:c + 1],
                                                       None, ALU.mult)
                    last.then_inc(u_diag, 1)
                    nc.vector.memset(dots[:, :], 0.0).then_inc(vectors_done, 1)

            dve.wait_ge(consts, 4)
            statistics0(0, 0)
            make_shift(0, 4)
            in_pairs(dve, NG, group0, peeled=2)

            def masked(q, at):
                at_least(dve, p_lo_done, at - NQ + q + 1)
                until(dve, mask_done, at + q + 1)
                s = slice(q * QW, (q + 1) * QW)
                nc.vector.tensor_tensor_reduce(out=score[:, s], in0=shared[:, s], in1=mask_sb[:, q % 2, :], scale=1.0,
                                               scalar=-3e38, op0=ALU.subtract, op1=ALU.max,
                                               accum_out=qmax[:, q:q + 1]).then_inc(z_done, 1)

            def quarters_max():
                return nc.vector.reduce_max(rowmax[:, 0:1], qmax[:, :], AX_X)

            def add_f1(n):
                dve.wait_ge(z_done, n * NQ + 1)
                nc.vector.tensor_scalar(score[:, 0:QW], score[:, 0:QW], f1[:, bass.ds(n, 1)], None,
                                        ALU.add).then_inc(y0_done, 1)

            def leaky(n, q):
                s = slice(q * QW, (q + 1) * QW)
                if q == 0:
                    dve.wait_ge(y0_done, n + 1)
                else:
                    dve.wait_ge(y_done, n * (NQ - 1) + q)
                nc.vector.scalar_tensor_tensor(out=score[:, s], in0=score[:, s], scalar=SLOPE, in1=score[:, s],
                                               op0=ALU.mult, op1=ALU.max).then_inc(leaky_done, 1)

            def p_lo(q, at):
                dve.wait_ge(p_hi_done, at + q + 1)
                nc.vector.scalar_tensor_tensor(out=p_nat[:, q % 2, 1, :], in0=score[:, q * QW:(q + 1) * QW],
                                               scalar=P_SCALE, in1=p_nat[:, q % 2, 0, :],
                                               op0=ALU.mult, op1=ALU.subtract).then_inc(p_lo_done, 1)

            def row_sum(n):
                dve.wait_ge(exp_done, n * NQ + NQ)
                nc.vector.tensor_tensor_reduce(out=qweighed[:, :], in0=qsum[:, :], in1=ones4[:, :],
                                               scale=P_SCALE * H_SCALE, scalar=0.0, op0=ALU.mult, op1=ALU.add,
                                               accum_out=rowsum[:, :]).then_inc(sum_chain, 1)

            def inverse_sum(n, r):
                dve.wait_ge(sum_chain, 2 * n + 1)
                nc.vector.reciprocal(rinv[:, r:r + 1], rowsum[:, :]).then_inc(sum_chain, 1)

            def residual0(n, r):
                dve.wait_ge(o_relu, n + 1)
                dve.wait_ge(xres_in[r], (n - r) * 8 + 16)
                nc.vector.tensor_tensor(xres[:, r, :], xres[:, r, :], work[:, :], ALU.add).then_inc(x1_done, 1)
                dve.wait_ge(x1_done, n + 1)
                nc.vector.bn_stats(stats[:, 0, :], xres[:, r, :]).then_inc(bn_done, 1)
                aggregate(NG + n, 1, n + (NT + 1))

            def products1(n):
                dve.wait_ge(h_hi_done, NT + n + 1)
                nc.vector.tensor_tensor(h_nat[:, 1, :], work[:, :], h_nat[:, 0, :], ALU.subtract).then_inc(h_lo_done, 1)
                dve.wait_ge(h_lo_done, NT + n + 1)
                dot(work[:, :], work[:, :], u_row[:, :], S_SCALE / H_SCALE, dots[:, :]).then_inc(h_used, 1)
                dve.wait_ge(h_used, n + 1)
                nc.vector.tensor_copy(u[:, bass.ds(n, 1)], dots[:, :]).then_inc(u_done, 1)

            tail = iter(range(V_TAIL + 3, NT))

            def spare(count=1):
                for _, v in zip(range(count), tail):
                    value_lo(v, v % 3)

            def layer0(n, r):
                first = isinstance(n, int) and n == 0
                early = isinstance(n, int) and n < 2
                last = isinstance(n, int) and n == NT - 1
                at = n * NQ
                if not first:
                    row_sum(n - 1)
                dve.wait_ge(z_done, at + NQ)
                quarters_max().then_inc(max_chain, 1)
                add_f1(n)
                dve.wait_ge(max_chain, 3 * n + 1)
                nc.vector.tensor_scalar(rowmax[:, 1:2], rowmax[:, 0:1], f1[:, bass.ds(n, 1)], -1.0,
                                        ALU.add, ALU.mult).then_inc(max_chain, 1)
                leaky(n, 0)
                dve.wait_ge(max_chain, 3 * n + 2)
                nc.vector.scalar_tensor_tensor(out=neg_max[:, :], in0=rowmax[:, 1:2], scalar=SLOPE,
                                               in1=rowmax[:, 1:2], op0=ALU.mult, op1=ALU.min).then_inc(max_chain, 1)
                if not first:
                    inverse_sum(n - 1, 1 - r)
                else:
                    spare()
                leaky(n, 1)
                leaky(n, 2)
                if first:
                    spare()
                leaky(n, 3)
                p_lo(0, at)
                if first:
                    spare()
                if not early:
                    residual0(n - 2, r)
                if not early:
                    make_shift(NG + n - 2, 1)
                p_lo(1, at)
                if first:
                    spare()
                if not last:
                    masked(0, at + NQ)
                p_lo(2, at)
                if first:
                    spare()
                if not last:
                    masked(1, at + NQ)
                if not early:
                    products1(n - 2)
                p_lo(3, at)
                if first:
                    spare()
                if not last:
                    masked(2, at + NQ)
                    masked(3, at + NQ)
                if first:
                    spare(NT)

            value_lo(*group_values(NG - 1)[2])
            last_values = [(n, n % 3) for n in range(V_TAIL, V_TAIL + 3)]
            value_lo(*last_values[0])
            dve.wait_ge(spread_used, NG)
            masked(0, 0)
            masked(1, 0)
            value_lo(*last_values[1])
            masked(2, 0)
            value_lo(*last_values[2])
            masked(3, 0)
            spare()
            dve.wait_ge(u_spread, 1)
            nc.vector.tensor_copy(u_row[:, :], ps_row[:, :]).then_inc(u_row_done, 1)

            in_pairs(dve, NT, layer0)

            row_sum(NT - 1)
            inverse_sum(NT - 1, 1)

            dve.wait_ge(w1_in, 2 * 16)
            dve.wait_ge(w_hi_done, 2)
            split_lo(w1_f32, W1_16[:, 0], W1_16[:, 1]).then_inc(w_split, 1)
            for n in range(NT - 2, NT):
                residual0(n, n % 2)
                make_shift(NG + n, 1)
                products1(n)
            dve.wait_ge(u_done, NT)
            nc.vector.tensor_scalar(u_row[:, :], vecs[:, 2, :], H_SCALE, None, ALU.mult).then_inc(bw_done, 1)
            nc.vector.tensor_scalar(u[:, :], u[:, :], bfbg[:, :], None, ALU.add).then_inc(u_done, 1)

            def bias_value(n, k):
                dve.wait_ge(v_ready, NT + n + 1)
                nc.vector.scalar_tensor_tensor(out=ps_v[1][k][:, :], in0=ps_v[1][k][:, :], scalar=1.0 / W_SCALE,
                                               in1=u_row[:, :], op0=ALU.mult, op1=ALU.add).then_inc(v_biased, 1)

            def value1(n, k):
                bias_value(n, k)
                value_lo(n, k, 1.0, 1)

            dve.wait_ge(bw_done, 1)

            def weight_lo(i):
                dve.wait_ge(w_hi_done, 3 + i)
                split_lo(wl[i], ws[:, 0], ws[:, 1]).then_inc(w_split, 1)

            def query_lo(g):
                for c in range(C):
                    dve.wait_ge(q_ready, g * C + c + 1)
                    nc.vector.tensor_scalar(query_bank(g, c), query_bank(g, c), Q_SCALE / (H_SCALE * W_SCALE),
                                            q_bias[:, c:c + 1], ALU.mult, ALU.add).then_inc(q_biased, 1)
                    dve.wait_ge(q_hi_done, g * C + c + 1)
                    nc.vector.tensor_tensor(q_lo[:, c, :], query_bank(g, c), q_hi[:, c, :],
                                            ALU.subtract).then_inc(q_lo_done, 1)

            B = NT * NQ

            def masked1(n):
                at = B + n * NQ
                for q in range(NQ):
                    dve.wait_ge(s_relu, n * NJ + (q + 1) * BQ)
                    until(dve, mask_done, at + q + 1)
                    s = slice(q * QW, (q + 1) * QW)
                    nc.vector.tensor_tensor_reduce(out=score[:, s], in0=score[:, s], in1=mask_sb[:, q % 2, :],
                                                   scale=1.0, scalar=-3e38, op0=ALU.subtract, op1=ALU.max,
                                                   accum_out=qmax[:, q:q + 1]).then_inc(z_done, 1)
                dve.wait_ge(z_done, at + NQ)
                quarters_max().then_inc(max_chain, 1)
                dve.wait_ge(max_chain, 3 * NT + 2 * n + 1)
                nc.vector.tensor_scalar(neg_max[:, :], rowmax[:, 0:1], -1.0 / S_SCALE, None,
                                        ALU.mult).then_inc(max_chain, 1)

            def final(n, r):
                dve.wait_ge(pv_done, B + n * NQ + NQ)
                dve.wait_ge(xres_in[r], NT // 2 * 16 + (n - r) * 8 + 16)
                nc.vector.scalar_tensor_tensor(out=xres[:, r, :], in0=ps_o[r][:, :], scalar=rinv[:, r:r + 1],
                                               in1=xres[:, r, :], op0=ALU.mult, op1=ALU.add).then_inc(y_final, 1)

            def layer1(n, r4, queries):
                for q in range(NQ):
                    v = V1_S + q
                    if isinstance(n, int) and n == 0:
                        bias_value(v, v % 3)
                    p_lo(q, B + n * NQ)
                    if isinstance(n, int) and n == 0:
                        value_lo(v, v % 3, 1.0, 1)
                row_sum(NT + n)
                inverse_sum(NT + n, r4 % 2)
                if not (isinstance(n, int) and n == 0):
                    final(n - 1, (r4 + 1) % 2)
                if not (isinstance(n, int) and n == NT - 1):
                    masked1(n + 1)
                if queries is not None:
                    query_lo(queries)

            in_threes(dve, 0, 6, value1)
            weight_lo(0)
            in_threes(dve, 6, 12, value1)
            weight_lo(1)
            in_threes(dve, 12, V1_M, value1)
            for c in range(C):
                dve.wait_ge(m_hi_done, c + 1)
                nc.vector.scalar_tensor_tensor(out=M_lo[:, c, :], in0=ps_s[c][:, :], scalar=1.0 / W_SCALE,
                                               in1=M_hi[:, c, :], op0=ALU.mult, op1=ALU.subtract).then_inc(m_lo_done, 1)
            in_threes(dve, V1_M, V1_Q, value1)
            query_lo(0)
            in_threes(dve, V1_Q, V1_S - 1, value1)
            value1(V1_S - 1, (V1_S - 1) % 3)
            masked1(0)
            for r in range(4):
                layer1(r, r, 1 if r == 2 else None)
            with dve.Fori(1, NT // 4 - 1, 1) as g:
                for r in range(4):
                    layer1(g * 4 + r, r, g + 1 if r == 2 else None)
            for r in range(4):
                layer1(NT - 4 + r, r, None)
            dve.wait_ge(sum_chain, 2 * 2 * NT)
            final(NT - 1, 1)

        @block.tensor
        def _(pe):
            def product(ps, a_hi, a_lo, b_hi, b_lo, start, stop):
                nc.tensor.matmul(ps, a_hi, b_hi, start=start, stop=False)
                nc.tensor.matmul(ps, a_hi, b_lo, start=False, stop=False)
                return nc.tensor.matmul(ps, a_lo, b_hi, start=False, stop=stop)

            def spread(g):
                pe.wait_ge(f_done, g + 1)
                at_least(pe, spread_used, g)
                nc.tensor.matmul(ps_row[:, :], pick_f2, f_rows, start=True, stop=True)
                for t in range(4):
                    last = nc.tensor.matmul(ps_col[:, t:t + 1], f_rows[:, t * P:(t + 1) * P], pick[0:4, 0:1],
                                            start=True, stop=True)
                last.then_inc(spread_out, 1)

            def values(n, k, layer, W):
                at_least(pe, v_lo_done, layer * NT + n - 2)
                rows_n = bass.ds(n * P, P)
                for c in range(C):
                    done = product(ps_v[layer][k][:, :], K_hi[:, c, rows_n], K_lo[:, c, rows_n], W[:, 0, c, :], W[:, 1, c, :],
                                   c == 0, c == C - 1)
                done.then_inc(v_ready, 1)

            def values0(n, k):
                values(n, k, 0, W0_16)

            def group0(g, g2):
                first = isinstance(g, int) and g == 0
                if not first:
                    for v in group_values(g):
                        values0(*v)
                for r in range(4):
                    pe.wait_ge(h0_out[4 * g2 + r], (g - g2) * 8 + 16)
                    if first and r == 0:
                        pe.wait_ge(w_split, 1)
                    if first and r < 3:
                        values0(*group_values(0)[r])
                if first:
                    pe.wait_ge(w12_done, 1)
                    pe.wait_ge(picks_done, 2)
                at_least(pe, f_done, g)
                cols = bass.ds(g * D, D)
                for c in range(C):
                    high = (ps_f[0:4, :], w12[:, c, :], K_hi[:, c, cols])
                    low = (ps_f[0:2, :], w12[:, c, 0:2], K_lo[:, c, cols])
                    if c < C - 1:
                        nc.tensor.matmul(*high, start=c == 0, stop=False)
                        nc.tensor.matmul(*low, start=False, stop=False)
                    else:
                        nc.tensor.matmul(*low, start=False, stop=False)
                        nc.tensor.matmul(*high, start=False, stop=True).then_inc(f_ready, 1)
                if not first:
                    spread(g - 1)

            in_pairs(pe, NG, group0)
            values0(V_TAIL, V_TAIL % 3)
            spread(NG - 1)
            values0(V_TAIL + 1, (V_TAIL + 1) % 3)
            pe.wait_ge(u_diag, 1)
            pe.wait_ge(spread_used, NG)
            nc.tensor.matmul(ps_row[:, :], ones, diag, start=True, stop=True).then_inc(u_spread, 1)
            in_threes(pe, V_TAIL + 2, NT - 2, values0)
            values0(NT - 2, 0)
            values0(NT - 1, 1)

            def weighted_values(n, r, at):
                for q in range(NQ):
                    pe.wait_ge(pt_in[q], at * 4 + 16)
                    if isinstance(at, int) and at == 0:
                        pe.wait_ge(v_lo_done, (q + 1) * JQ)
                    for j in range(q * JQ, (q + 1) * JQ):
                        last = product(ps_o[r][:, :], PT[:, q, 0, j % JQ, :], PT[:, q, 1, j % JQ, :],
                                       V_hi[:, j, :], V_lo[:, j, :], j == 0, j == NT - 1)
                    last.then_inc(pv_done, 1)

            def layer0(n, r):
                at_least(pe, o_relu, n - 1)
                weighted_values(n, r, n * NQ)

            in_pairs(pe, NT, layer0)

            pe.wait_ge(w_split, 2)

            def values1(n, k):
                pe.wait_ge(h_hi_done, NT + n + 2)
                values(n, k, 1, W1_16)

            values1(0, 0)
            values1(1, 1)
            pe.wait_ge(o_relu, NT - 1)
            values1(2, 2)
            in_threes(pe, 3, V1_M, values1)
            for i in range(2):
                pe.wait_ge(wt_in[i], 8 * 16)
            for d in range(C):
                for c in range(C):
                    k = slice(d * P, (d + 1) * P)
                    last = product(ps_s[d][:, :], sh16[:, 0, 0, c, k], sh16[:, 0, 1, c, k],
                                   sh16[:, 1, 0, c, :], sh16[:, 1, 1, c, :], c == 0, c == C - 1)
                last.then_inc(m_ready, 1)
            in_threes(pe, V1_M, V1_Q, values1)

            def query(g):
                for d in range(C):
                    at_least(pe, q_lo_done, g * C + d - 1 if not isinstance(g, int) or g > 1 or d > 1 else 0)
                    for c in range(C):
                        k = slice(d * P, (d + 1) * P)
                        i = bass.ds(g * D, D)
                        last = product(query_bank(g, d), M_hi[:, c, k], M_lo[:, c, k], K_hi[:, c, i], K_lo[:, c, i],
                                       c == 0, c == C - 1)
                    last.then_inc(q_ready, 1)

            def scores(n, r4, g):
                pe.wait_ge(q_lo_done, g * C + C)
                for j in range(NJ):
                    at_least(pe, s_relu, n * NJ + j - 3)
                    i = slice(r4 * P, (r4 + 1) * P)
                    k = slice(j * JB, (j + 1) * JB)
                    for c in range(C):
                        last = product(ps_s[j % 4][:, :], q_hi[:, c, i], q_lo[:, c, i], K_hi[:, c, k], K_lo[:, c, k],
                                       c == 0, c == C - 1)
                    last.then_inc(s_ready, 1)

            pe.wait_ge(m_lo_done, C)
            query(0)
            in_threes(pe, V1_Q, V1_S - 1, values1)
            values1(V1_S - 1, (V1_S - 1) % 3)
            pe.wait_ge(h1_out, NT * 16)
            pe.wait_ge(w1_moved, 16)
            scores(0, 0, 0)
            for n in range(V1_S, NT):
                values(n, n % 3, 1, W0_16)

            def layer1(n, r4, g, queries):
                if not (isinstance(n, int) and n == NT - 1):
                    scores(n + 1, (r4 + 1) % 4, g + 1 if r4 == 3 else g)
                if isinstance(n, int) and n == 0:
                    pe.wait_ge(v_lo_done, 2 * NT)
                if queries is not None:
                    query(queries)
                at_least(pe, y_final, n - 1)
                weighted_values(n, r4 % 2, NT * NQ + n * NQ)

            for r in range(4):
                layer1(r, r, 0, 1 if r == 2 else None)
            with pe.Fori(1, NT // 4 - 1, 1) as g:
                for r in range(4):
                    layer1(g * 4 + r, r, g, g + 1 if r == 2 else None)
            for r in range(4):
                layer1(NT - 4 + r, r, NT // 4 - 1, None)


_INS = ['x', 'adj', 'L0_gnn_W', 'L0_gnn_a1', 'L0_gnn_a2', 'L1_gnn_Wf', 'L1_gnn_bf', 'L1_gnn_Wg', 'L1_gnn_bg',
        'L1_gnn_W', 'L1_gnn_bW']


def kernel(**inputs):
    import numpy as _np
    import concourse.bacc as _bacc
    from concourse import mybir as _mybir
    from concourse.bass_utils import run_bass_kernel_spmd as _run

    nc = _bacc.Bacc("TRN2", target_bir_lowering=False, num_devices=1)
    arrays, args = {}, []
    for name in _INS:
        a = _np.ascontiguousarray(inputs[name])
        arrays[f"in_{name}_dram"] = a
        args.append(nc.dram_tensor(f"in_{name}_dram", a.shape, _mybir.dt.from_np(a.dtype), kind="ExternalInput").ap())
    out = nc.dram_tensor("out_dram", inputs['x'].shape, _mybir.dt.float32, kind="ExternalOutput").ap()
    graph_layers(nc, *args, out)
    r = _run(nc, [arrays], core_ids=[0])
    return r.results[0]["out_dram"]
```
